# Optimizing a Trainium2 kernel written in Bass

```python
import numpy as np
import jax
import jax.numpy as jnp

def _softmax(x, axis=-1):
    return jax.nn.softmax(x, axis=axis)

def _gelu(x):
    return jax.nn.gelu(x, approximate=True)

def _silu(x):
    return jax.nn.silu(x)

def _sigmoid(x):
    return jax.nn.sigmoid(x)

def _layernorm(x, axis=-1, eps=1e-05):
    m = jnp.mean(x, axis=axis, keepdims=True)
    v = jnp.var(x, axis=axis, keepdims=True)
    return (x - m) / jnp.sqrt(v + eps)

def _scatter_add(tgt, idx, src, axis=0):
    return tgt.at[idx].add(src)

def _segment_sum(src, seg, n):
    return jax.ops.segment_sum(src, seg, n)
kernel_name = 'mk_seq_preln_d1_jaxref_r8_c82277'

def setup_inputs(seed: int=0):
    np.random.seed(seed)
    _w = jnp.asarray

    def _L0_attn_setup():
        import jax, jax.numpy as jnp
        import numpy as np
        D_ATT_IN = 128
        NUM_HEADS = 16
        D_Q = 64
        D_V = 64
        D_MODEL = 128

        def _trunc_normal(key, shape, std):
            return jax.random.truncated_normal(key, -3.0, 3.0, shape, dtype=jnp.float32) * std
        key = jax.random.key(seed)
        k_x, k_q, k_k, k_v, k_o = jax.random.split(key, 5)

        def init_w(k, out_f, in_f):
            s = np.sqrt(2.0 / (in_f + out_f))
            return _trunc_normal(k, (out_f, in_f), s)
        return {'in_features': jax.random.normal(k_x, (4, 256, D_ATT_IN), dtype=jnp.float32), 'w_q': init_w(k_q, NUM_HEADS * D_Q, D_ATT_IN), 'w_k': init_w(k_k, NUM_HEADS * D_Q, D_ATT_IN), 'w_v': init_w(k_v, NUM_HEADS * D_V, D_ATT_IN), 'w_o': init_w(k_o, D_MODEL, NUM_HEADS * D_V)}
    _L0_attn_in = _L0_attn_setup()

    def _L0_ffn_setup():
        import jax, jax.numpy as jnp
        import numpy as np
        E, K, D, H = (8, 2, 128, 256)
        B, S = (1, 128)

        def _grouped_swiglu(x_sorted, counts, w1, w2, w3):
            if hasattr(jax.lax, 'ragged_dot'):
                gs = counts.astype(jnp.int32)
                h = jax.nn.silu(jax.lax.ragged_dot(x_sorted, w1, gs)) * jax.lax.ragged_dot(x_sorted, w3, gs)
                return jax.lax.ragged_dot(h, w2, gs)
            pos = jnp.arange(x_sorted.shape[0])
            eid = jnp.searchsorted(jnp.cumsum(counts), pos, side='right')
            out = jnp.zeros((x_sorted.shape[0], w2.shape[-1]), x_sorted.dtype)
            for e in range(w1.shape[0]):
                xm = jnp.where((eid == e)[:, None], x_sorted, 0.0)
                he = jax.nn.silu(xm @ w1[e]) * (xm @ w3[e])
                out = out + he @ w2[e]
            return out
        key = jax.random.key(seed)
        k0, k1, k2, k3, k4 = jax.random.split(key, 5)
        sD = 1.0 / np.sqrt(D)
        sH = 1.0 / np.sqrt(H)
        return {'hidden_states': jax.random.normal(k0, (B, S, D), jnp.float32), 'gate_w': jax.random.normal(k1, (E, D), jnp.float32) * sD, 'w1': jax.random.normal(k2, (E, D, H), jnp.float32) * sD, 'w2': jax.random.normal(k3, (E, H, D), jnp.float32) * sH, 'w3': jax.random.normal(k4, (E, D, H), jnp.float32) * sD}
    _L0_ffn_in = _L0_ffn_setup()
    _d = {'L0_attn_in_features': _L0_attn_in['in_features'], 'L0_attn_w_q': _L0_attn_in['w_q'], 'L0_attn_w_k': _L0_attn_in['w_k'], 'L0_attn_w_v': _L0_attn_in['w_v'], 'L0_attn_w_o': _L0_attn_in['w_o'], 'L0_ffn_gate_w': _L0_ffn_in['gate_w'], 'L0_ffn_w1': _L0_ffn_in['w1'], 'L0_ffn_w2': _L0_ffn_in['w2'], 'L0_ffn_w3': _L0_ffn_in['w3']}
    _x0 = _d['L0_attn_in_features']
    _d['L0_attn_in_features'] = jax.random.normal(jax.random.fold_in(jax.random.key(seed), 1), (4, 1024, 128), dtype=_x0.dtype)
    del _x0
    return _d

def reference(L0_attn_in_features, L0_attn_w_q, L0_attn_w_k, L0_attn_w_v, L0_attn_w_o, L0_ffn_gate_w, L0_ffn_w1, L0_ffn_w2, L0_ffn_w3):

    def _L0_attn_ref(in_features, w_q, w_k, w_v, w_o):
        import jax, jax.numpy as jnp
        import numpy as np
        D_ATT_IN = 128
        NUM_HEADS = 16
        D_Q = 64
        D_V = 64
        D_MODEL = 128

        def _trunc_normal(key, shape, std):
            return jax.random.truncated_normal(key, -3.0, 3.0, shape, dtype=jnp.float32) * std
        q = jnp.einsum('oi,bsi->bso', w_q, in_features)
        k = jnp.einsum('oi,bsi->bso', w_k, in_features)
        v = jnp.einsum('oi,bsi->bso', w_v, in_features)
        s = in_features.shape[-2]
        scores = jnp.einsum('bqd,bkd->bqk', q, k) / jnp.sqrt(jnp.asarray(k.shape[-1], q.dtype))
        causal = jnp.tril(jnp.ones((s, s), dtype=bool))
        scores = jnp.where(causal[None, :, :], scores, -jnp.inf)
        att = jax.nn.softmax(scores, axis=-1)
        ctx = jnp.einsum('bqk,bkd->bqd', att, v)
        return jnp.einsum('oi,bsi->bso', w_o, ctx)

    def _L0_ffn_ref(hidden_states, gate_w, w1, w2, w3):
        import jax, jax.numpy as jnp
        import numpy as np
        E, K, D, H = (8, 2, 128, 256)
        B, S = (1, 128)

        def _grouped_swiglu(x_sorted, counts, w1, w2, w3):
            if hasattr(jax.lax, 'ragged_dot'):
                gs = counts.astype(jnp.int32)
                h = jax.nn.silu(jax.lax.ragged_dot(x_sorted, w1, gs)) * jax.lax.ragged_dot(x_sorted, w3, gs)
                return jax.lax.ragged_dot(h, w2, gs)
            pos = jnp.arange(x_sorted.shape[0])
            eid = jnp.searchsorted(jnp.cumsum(counts), pos, side='right')
            out = jnp.zeros((x_sorted.shape[0], w2.shape[-1]), x_sorted.dtype)
            for e in range(w1.shape[0]):
                xm = jnp.where((eid == e)[:, None], x_sorted, 0.0)
                he = jax.nn.silu(xm @ w1[e]) * (xm @ w3[e])
                out = out + he @ w2[e]
            return out
        x = hidden_states.reshape(-1, D)
        N = x.shape[0]
        scores = jax.nn.softmax(x @ gate_w.T, axis=-1)
        top_scores, sel = jax.lax.top_k(scores, K)
        sel_flat = sel.T.reshape(-1)
        scores_flat = top_scores.T.reshape(-1)
        order = jnp.argsort(sel_flat, stable=True)
        tok_sorted = order % N
        scores_sorted = scores_flat[order]
        counts = jnp.bincount(sel_flat, length=E)
        x_sorted = x[tok_sorted]
        y = _grouped_swiglu(x_sorted, counts, w1, w2, w3)
        weighted = y * scores_sorted[:, None]
        out = jnp.zeros((N, D), x.dtype).at[tok_sorted].add(weighted)
        return out.reshape(hidden_states.shape)
    x = L0_attn_in_features
    x = x + _L0_attn_ref(_layernorm(x, axis=-1), L0_attn_w_q, L0_attn_w_k, L0_attn_w_v, L0_attn_w_o)
    x = x + _L0_ffn_ref(_layernorm(x, axis=-1), L0_ffn_gate_w, L0_ffn_w1, L0_ffn_w2, L0_ffn_w3)
    return x

_drawn_inputs = setup_inputs


def setup_inputs(seed=0):
    import zlib

    import numpy as np

    out = dict(_drawn_inputs(seed))
    spreads = {}
    factors = {}
    for name, (base, spread) in spreads.items():
        noise = np.random.default_rng([zlib.crc32(name.encode()), seed]).standard_normal(out[name].shape)
        drawn = base * np.exp(spread * noise) if base else spread * noise
        out[name] = jnp.asarray(drawn.astype(out[name].dtype))
    for name, factor in factors.items():
        out[name] = (out[name] * factor).astype(out[name].dtype)
    return out
```

```python
from contextlib import ExitStack

import numpy as np

import concourse.bass as bass
from concourse import mybir

P = 128
B, S, D = 4, 1024, 128
E, H, K = 8, 256, 2
F_ATT = 1024
EPS = 1e-5
N_TOK = B * S
QT = S // P
PAIR = 2
ITERS = B // PAIR
NU = PAIR * QT
FC = F_ATT // P
GRP = 4
NG = NU // GRP
ROW = D + 4
COL_DEST, COL_W = D, D + 1
STRETCH = N_TOK + P
LANES = 4
MOST_TILES = (K * N_TOK + E * (P - 1)) // P
NT = -(-MOST_TILES // LANES) * LANES
SPARE = NT - K * N_TOK // P
XS_ROWS = E * STRETCH + SPARE * P
YB_ROWS = K * N_TOK + (E + SPARE) * P
MASK = -3.0e38

N_CONST = 10 + K

XT_LEAD, TV_LEAD, S_LEAD = 3, 2, 1
STAT1_LEAD, NORM1_LEAD = 6, 4
PV_LAG, X1_LAG, NORM2_LAG, X2T_LAG, L_LAG, TOP_LAG = 1, 2, 3, 4, 5, 6
ROUTE_LAG, RANK_LAG, PLACE_LAG = 9, 10, 11


def build(nc, x, w_q, w_k, w_v, w_o, gate_w, w1, w2, w3, out):
    f32, bf16 = mybir.dt.float32, mybir.dt.bfloat16
    i32, u32 = mybir.dt.int32, mybir.dt.uint32
    ALU, ACT, AX = mybir.AluOpType, mybir.ActivationFunctionType, mybir.AxisListType
    ds = bass.ds

    xs = nc.dram_tensor("expert_rows", (XS_ROWS, ROW), f32, kind="Internal").ap()
    yb = nc.dram_tensor("choice_rows", (YB_ROWS, D), f32, kind="Internal").ap()

    ctx = ExitStack()
    with ctx:
        def sb(name, shape, dt=f32):
            return ctx.enter_context(nc.sbuf_tensor(name, shape, dt))

        def pb(name):
            return ctx.enter_context(nc.psum_tensor(name, [P, 512], f32))

        def sem(name):
            return ctx.enter_context(nc.semaphore(name))

        X = sb("X", [P, N_TOK // P, D])
        wq_sb, wk_sb, wv_sb = (sb(n, [P, FC, D]) for n in ("wq_sb", "wk_sb", "wv_sb"))
        wo_sb = sb("wo_sb", [P, F_ATT])
        woT = sb("woT", [P, FC, P])
        A_sb, M_sb = sb("A_sb", [P, P]), sb("M_sb", [P, P])
        gw_sb, gwT = sb("gw_sb", [E, D]), sb("gwT", [P, E])
        w13 = sb("w13", [P, E, 2 * H])
        w2_sb = sb("w2_sb", [P, E, H // P, D])
        identf, identb = sb("identf", [P, P]), sb("identb", [P, P], bf16)
        maskb = sb("maskb", [P, P], bf16)
        before = sb("before", [P, P], bf16)
        onesb = sb("onesb", [P, P], bf16)
        halves = sb("halves", [P, 2])
        iota8 = sb("iota8", [P, E])
        stretch0 = sb("stretch0", [P, E])
        dests = sb("dests", [P, ITERS, PAIR, QT, K])
        xn = sb("xn", [P, 4, D])
        XX = sb("XX", [P, NU + X2T_LAG + XT_LEAD, 2, P])
        TL = sb("TL", [P, NU + L_LAG + TV_LEAD, 2 * P + E])
        Pr = sb("Pr", [P, 2, S])
        PT = sb("PT", [P, 2, S])
        negmax, rowsum, rinv = sb("negmax", [P, 4]), sb("rowsum", [P, 4]), sb("rinv", [P, 4])
        bn = sb("bn", [P, 2, 2, 6])
        mv = sb("mv", [P, 4, 2, 2])
        ve = sb("ve", [P, 4, 2])
        rstd = sb("rstd", [P, 4, 2])
        rows = sb("rows", [P, NU, K, ROW])
        top = sb("top", [P, 2, GRP, 8])
        topi = sb("topi", [P, 2, GRP, 8], u32)
        dlog, elog = sb("dlog", [P, GRP, 8]), sb("elog", [P, GRP, 8])
        esum, einv = sb("esum", [P, GRP]), sb("einv", [P, GRP])
        hot = sb("hot", [P, GRP, K, E], bf16)
        chosen = sb("chosen", [P, GRP, E], bf16)
        newc = sb("newc", [P, E], bf16)
        seen = sb("seen", [P, E], bf16)
        place, picked = sb("place", [P, GRP, E]), sb("picked", [P, GRP, K, E])
        slots = sb("slots", [P, NG * GRP, K], u32)
        cnt, cnti = sb("cnt", [1, E]), sb("cnti", [1, E], i32)
        nti, ntf, zero8, ntcum = sb("nti", [1, E], i32), sb("ntf", [1, E]), sb("zero8", [1, E]), sb("ntcum", [1, E])
        pad0 = sb("pad0", [1, E], i32)
        iotat = sb("iotat", [1, NT])
        past, pastn = sb("past", [1, NT, E]), sb("pastn", [1, NT, E])
        e_of, s_of, r_of = sb("e_of", [1, NT]), sb("s_of", [1, NT]), sb("r_of", [1, NT])
        row0, eidx = sb("row0", [1, NT], i32), sb("eidx", [1, NT], i32)
        padrows = sb("padrows", [P, E + SPARE, ROW])
        xt = sb("xt", [P, LANES, ROW])
        xTs = sb("xTs", [P, 2, P])
        sil, g = sb("sil", [P, 2, H]), sb("g", [P, 2, H])
        gTs = sb("gTs", [P, 2, H])
        ysb, ydest = sb("ysb", [P, LANES, D]), sb("ydest", [P, LANES], u32)
        FIN = 4
        NF = N_TOK // P // FIN
        yf = sb("yf", [P, 2, K, FIN, D])

        pS = [ctx.enter_context(nc.psum_tensor(f"scores{i}", [P, 1024], f32)) for i in range(2)]
        pT, (pM, pO) = [pb("turned0"), pb("turned1")], [pb("mixed"), pb("weighed")]
        bank = [pS[0][:, 0:512], pS[0][:, 512:], pS[1][:, 0:512], pS[1][:, 512:], *pT, pM, pO]

        x_head, x_mid, x_tail, x_in = sem("x_head"), sem("x_mid"), sem("x_tail"), sem("x_in")
        rows_free = sem("rows_free")
        wqk_in, wv_in, wo_in, gw_in, w_in = sem("wqk_in"), sem("wv_in"), sem("wo_in"), sem("gw_in"), sem("w_in")
        held = sem("held")
        const0, consts = sem("const0"), sem("consts")
        A_mm, woT_mm, M_mm, gwT_mm = sem("A_mm"), sem("woT_mm"), sem("M_mm"), sem("gwT_mm")
        A_rdy, woT_rdy, M_rdy, gwT_rdy = sem("A_rdy"), sem("woT_rdy"), sem("M_rdy"), sem("gwT_rdy")
        bn_rdy, mv_rdy, ve_rdy, rstd_rdy = sem("bn_rdy"), sem("mv_rdy"), sem("ve_rdy"), sem("rstd_rdy")
        xn_rdy, xx_mm, xx_ev, tl_mm, tl_ev = sem("xn_rdy"), sem("xx_mm"), sem("xx_ev"), sem("tl_mm"), sem("tl_ev")
        s_mm, max_rdy, p_rdy = sem("s_mm"), sem("max_rdy"), sem("p_rdy")
        pt_mm, pt_ev, pv_mm, rinv_rdy, x1_rdy = sem("pt_mm"), sem("pt_ev"), sem("pv_mm"), sem("rinv_rdy"), sem("x1_rdy")
        x2_rdy, top_rdy, topi_rdy = sem("x2_rdy"), sem("top_rdy"), sem("topi_rdy")
        dlog_rdy, elog_rdy, hot_rdy, chosen_rdy = sem("dlog_rdy"), sem("elog_rdy"), sem("hot_rdy"), sem("chosen_rdy")
        newc_rdy, seen_rdy, rank_mm, place_rdy, picked_rdy = sem("newc_rdy"), sem("seen_rdy"), sem("rank_mm"), sem("place_rdy"), sem("picked_rdy")
        esum_rdy, einv_rdy, row_rdy, scattered = sem("esum_rdy"), sem("einv_rdy"), sem("row_rdy"), sem("scattered")
        cnt_mm, listing, list_rdy, padded = sem("cnt_mm"), sem("listing"), sem("list_rdy"), sem("padded")
        xt_in = [sem(f"xt_in{j}") for j in range(LANES)]
        y_out = [sem(f"y_out{j}") for j in range(LANES)]
        xT_mm, xT_rdy, h_mm, sil_rdy, g_rdy = sem("xT_mm"), sem("xT_rdy"), sem("h_mm"), sem("sil_rdy"), sem("g_rdy")
        gT_mm, gT_rdy, y_mm, y_rdy = sem("gT_mm"), sem("gT_rdy"), sem("y_mm"), sem("y_rdy")
        yf_in = [sem(f"yf_in{j}") for j in range(2)]
        sum0, sum1, out_done = sem("sum0"), sem("sum1"), sem("out_done")

        XXN = NU + X2T_LAG + XT_LEAD
        TLN = NU + L_LAG + TV_LEAD
        STN = NU + STAT1_LEAD + X1_LAG
        BNN = 2 * NU

        def chunks(u):
            return sum(-(-(v // PAIR + 1) // 4) for v in range(u))

        CHN = chunks(NU)

        def is_tile(u):
            return 0 <= u < NU

        def after(eng, semaphore, it, per_iter, count):
            eng.wait_ge(semaphore, it * per_iter + max(count, 0) + 1)

        def alone(eng):
            eng.sem_inc(held, 1)

        def token_tile(it, u):
            return it * NU + (u % PAIR) * QT + u // PAIR

        looped = [bn_rdy, mv_rdy, ve_rdy, rstd_rdy, xn_rdy, xx_mm, xx_ev, tl_mm, tl_ev, s_mm, max_rdy, p_rdy,
                  pt_mm, pt_ev, pv_mm, rinv_rdy, x1_rdy, x2_rdy, top_rdy, topi_rdy, dlog_rdy, elog_rdy, hot_rdy,
                  chosen_rdy, newc_rdy, seen_rdy, rank_mm, place_rdy, picked_rdy, esum_rdy, einv_rdy, row_rdy,
                  rows_free]

        block = ctx.enter_context(nc.Block())

        @block.sync
        def _(sp):
            xv = x.rearrange("b (i p) d -> p b i d", p=P)
            Xv = X[:, :, :].rearrange("p (b i) d -> p b i d", b=B)
            for b in range(PAIR):
                sp.dma_start(Xv[:, b, 0:2, :], xv[:, b, 0:2, :]).then_inc(x_head, 16)
            sp.dma_start(wq_sb[:, :, :], w_q.rearrange("(c p) i -> p c i", p=P)).then_inc(wqk_in, 16)
            sp.dma_start(wk_sb[:, :, :], w_k.rearrange("(c p) i -> p c i", p=P)).then_inc(wqk_in, 16)
            sp.dma_start(wo_sb[:, :], w_o).then_inc(wo_in, 16)
            sp.dma_start(wv_sb[:, :, :], w_v.rearrange("(c p) i -> p c i", p=P)).then_inc(wv_in, 16)
            sp.dma_start(gw_sb[:, :], gate_w).then_inc(gw_in, 16)
            for b in range(PAIR):
                sp.dma_start(Xv[:, b, 2:QT, :], xv[:, b, 2:QT, :]).then_inc(x_mid, 16)
            for b in range(PAIR, B):
                sp.dma_start(Xv[:, b, :, :], xv[:, b, :, :]).then_inc(x_tail, 16)
            sp.dma_start(w13[:, :, 0:H], w1.rearrange("e p h -> p e h")).then_inc(w_in, 16)
            sp.dma_start(w13[:, :, H:2 * H], w3.rearrange("e p h -> p e h")).then_inc(w_in, 16)
            sp.dma_start(w2_sb[:, :, :, :].rearrange("p e t d -> p (e t) d"),
                         w2.rearrange("e (t p) d -> p (e t) d", p=P)).then_inc(w_in, 16)
            for semaphore in looped:
                sp.sem_inc(semaphore, 1)
            sp.wait_ge(x_head, 32)
            sp.sem_inc(x_in, 1)
            sp.wait_ge(x_tail, 32)
            sp.sem_inc(x_in, 1)
            for n in range(ITERS - 1):
                sp.wait_ge(scattered, 16 * K * NU * (n + 1))
                sp.sem_inc(rows_free, 1)
            sp.wait_ge(list_rdy, 1)
            sp.wait_ge(scattered, 16 * K * NU * ITERS)
            for e in range(E):
                r = sp.value_load(pad0[0:1, e:e + 1], min_val=e * STRETCH, max_val=e * STRETCH + N_TOK)
                sp.dma_start(xs[ds(r, P), :], padrows[:, e, :]).then_inc(padded, 16)
            sp.dma_start(xs[E * STRETCH:XS_ROWS, :].rearrange("(j p) c -> p j c", p=P),
                         padrows[:, E:, :]).then_inc(padded, 16)
            sp.wait_ge(padded, 16 * (E + 1))

            def load(m, j):
                t = m * LANES + j
                if not isinstance(t, int) or t >= LANES:
                    sp.wait_ge(xT_mm, t - LANES + 1)
                    sp.wait_ge(y_rdy, t - LANES + 1)
                r = sp.value_load(row0[0:1, ds(t, 1)], min_val=0, max_val=XS_ROWS - P)
                sp.dma_start(xt[:, j, :], xs[ds(r, P), :]).then_inc(xt_in[j], 16)

            for j in range(LANES):
                load(0, j)
            with sp.Fori(1, NT // LANES) as m:
                for j in range(LANES):
                    load(m, j)

            for j in range(LANES):
                sp.wait_ge(y_out[j], 16 * (NT // LANES))
            yv = yb[0:K * N_TOK, :].rearrange("(k c i p) d -> p k c i d", k=K, c=NF, i=FIN)
            ov = out.rearrange("b (c i p) d -> (b c) p i d", c=NF // B, i=FIN)

            def fetch(c):
                for k in range(K):
                    sp.dma_start(yf[:, c % 2, k, :, :], yv[:, k, c, :, :]).then_inc(yf_in[c % 2], 16)

            fetch(0)
            for c in range(NF):
                if c + 1 < NF:
                    if c >= 1:
                        sp.wait_ge(sum1, c)
                    fetch(c + 1)
                sp.wait_ge(sum1, c + 1)
                sp.dma_start(ov[c], X[:, c * FIN:(c + 1) * FIN, :]).then_inc(out_done, 16)
            sp.wait_ge(out_done, 16 * NF)

        @block.gpsimd
        def _(pool):
            nc.gpsimd.memset(identf[:, :], 0.0).then_inc(const0, 1)
            nc.gpsimd.memset(maskb[:, :], 0.0).then_inc(const0, 1)
            nc.gpsimd.memset(onesb[:, :], 1.0).then_inc(const0, 1)
            pool.wait_ge(const0, 3)
            nc.gpsimd.affine_select(out=identf[:, :], in_=identf[:, :], compare_op=ALU.not_equal, fill=1.0,
                                    base=0, pattern=[[-1, P]], channel_multiplier=1).then_inc(const0, 1)
            nc.gpsimd.affine_select(out=maskb[:, :], in_=maskb[:, :], compare_op=ALU.is_ge, fill=MASK,
                                    base=0, pattern=[[-1, P]], channel_multiplier=1).then_inc(const0, 1)
            nc.gpsimd.affine_select(out=before[:, :], in_=onesb[:, :], compare_op=ALU.is_gt, fill=0.0,
                                    base=0, pattern=[[1, P]], channel_multiplier=-1).then_inc(const0, 1)
            pool.wait_ge(const0, 6)
            nc.gpsimd.tensor_copy(identb[:, :], identf[:, :]).then_inc(consts, 1)
            nc.gpsimd.memset(halves[:, :], -0.5).then_inc(consts, 1)
            nc.gpsimd.iota(iota8[:, :], [[1, E]], base=0, channel_multiplier=0,
                           allow_small_or_imprecise_dtypes=True).then_inc(consts, 1)
            nc.gpsimd.iota(stretch0[:, :], [[STRETCH, E]], base=0, channel_multiplier=0,
                           allow_small_or_imprecise_dtypes=True).then_inc(consts, 1)
            for k in range(K):
                nc.gpsimd.iota(dests[:, :, :, :, k].bitcast(u32), [[NU * P, ITERS], [S, PAIR], [P, QT]], base=k * N_TOK,
                               channel_multiplier=1).then_inc(consts, 1)
            nc.gpsimd.memset(seen[:, :], 0.0).then_inc(consts, 1)
            nc.gpsimd.iota(iotat[:, :], [[1, NT]], base=0, channel_multiplier=0,
                           allow_small_or_imprecise_dtypes=True).then_inc(consts, 1)
            nc.gpsimd.memset(zero8[:, :], 0.0).then_inc(consts, 1)
            nc.gpsimd.memset(rows[:, :, :, D:ROW], 0.0).then_inc(consts, 1)
            nc.gpsimd.memset(padrows[:, :, :], 0.0).then_inc(consts, 1)
            pool.wait_ge(consts, N_CONST - 1)
            nc.gpsimd.iota(padrows[:, :, COL_DEST].bitcast(u32), [[P, E + SPARE]], base=K * N_TOK,
                           channel_multiplier=1).then_inc(consts, 1)

            def rstd_of(it, s):
                kinds = slice(0 if is_tile(s + STAT1_LEAD) else 1, 2 if is_tile(s - X1_LAG) else 1)
                n = s + STAT1_LEAD + 1
                after(pool, mv_rdy, it, STN, n)
                alone(pool)
                nc.gpsimd.tensor_scalar_add(ve[:, s % 4, kinds], mv[:, s % 4, kinds, 1], EPS).then_inc(ve_rdy, 1)
                after(pool, ve_rdy, it, STN, n)
                nc.gpsimd.tensor_tensor(rstd[:, s % 4, kinds], ve[:, s % 4, kinds], halves[:, kinds],
                                        ALU.pow).then_inc(rstd_rdy, 1)

            def scatter(it, gr):
                after(pool, row_rdy, it, NG, gr + 1)
                alone(pool)
                for a in range(GRP):
                    for k in range(K):
                        nc.gpsimd.indirect_dma_start(
                            xs, bass.IndirectOffsetOnAxis(ap=slots[:, gr * GRP + a, k:k + 1], axis=0),
                            rows[:, gr * GRP + a, k, :], None).then_inc(scattered, 16)

            with pool.Fori(0, ITERS) as it:
                for s in range(-STAT1_LEAD, NU + PLACE_LAG):
                    if is_tile(s + STAT1_LEAD) or is_tile(s - X1_LAG):
                        rstd_of(it, s)
                    if (s - PLACE_LAG - 1) % GRP == 0 and 0 <= (s - PLACE_LAG - 1) // GRP < NG - 1:
                        scatter(it, (s - PLACE_LAG - 1) // GRP)
                scatter(it, NG - 1)

            def store(m, j):
                t = m * LANES + j
                pool.wait_ge(y_rdy, t + 1)
                alone(pool)
                nc.gpsimd.indirect_dma_start(
                    yb, bass.IndirectOffsetOnAxis(ap=ydest[:, j:j + 1], axis=0),
                    ysb[:, j, :], None).then_inc(y_out[j], 16)

            with pool.Fori(0, NT // LANES) as m:
                for j in range(LANES):
                    store(m, j)

        @block.tensor
        def _(pe):
            mm = nc.tensor.matmul
            pe.wait_ge(consts, N_CONST)
            pe.wait_ge(wo_in, 16)
            for c in range(FC):
                nc.tensor.transpose(pT[c // 4][:, c % 4 * P:(c % 4 + 1) * P], wo_sb[:, c * P:(c + 1) * P],
                                    identf[:, :]).then_inc(woT_mm, 1)
            pe.wait_ge(wqk_in, 32)
            for c in range(FC):
                i = mm(pS[0][:, 0:P], wq_sb[:, c, :], wk_sb[:, c, :], start=c == 0, stop=c == FC - 1)
            i.then_inc(A_mm, 1)
            pe.wait_ge(gw_in, 16)
            nc.tensor.transpose(pO[:, 0:E], gw_sb[:, :], identf[0:E, 0:E]).then_inc(gwT_mm, 1)
            pe.wait_ge(wv_in, 16)
            pe.wait_ge(woT_rdy, 2)
            for c in range(FC):
                i = mm(pS[1][:, 0:P], wv_sb[:, c, :], woT[:, c, :], start=c == 0, stop=c == FC - 1)
            i.then_inc(M_mm, 1)
            pe.wait_ge(A_rdy, 1)
            pe.wait_ge(M_rdy, 1)
            pe.wait_ge(gwT_rdy, 1)

            def transposes(it, s):
                if s == -XT_LEAD:
                    after(pe, place_rdy, it, NG, 0)
                elif s == -XT_LEAD + 1:
                    after(pe, xx_ev, it, XXN, 1)
                else:
                    after(pe, tl_ev, it, TLN, s + TV_LEAD)
                if s - 1 >= RANK_LAG and (s - 1 - RANK_LAG) % GRP == 0:
                    after(pe, place_rdy, it, NG, (s - 1 - RANK_LAG) // GRP + 1)
                u, v = s + XT_LEAD, s - X2T_LAG
                if is_tile(u):
                    after(pe, xn_rdy, it, NU, u + 1)
                    i = nc.tensor.transpose(pM[:, 0:P], xn[:, u % 4, :], identf[:, :])
                if is_tile(v):
                    after(pe, x2_rdy, it, NU, v + 1)
                    i = nc.tensor.transpose(pM[:, P:2 * P], rows[:, v, 0, 0:D], identf[:, :])
                i.then_inc(xx_mm, 1)

            def scores(it, u):
                after(pe, p_rdy, it, NU, u - 1)
                after(pe, tl_ev, it, TLN, u + 1)
                i, h = u // PAIR, u % PAIR
                w = (i + 1) * P
                q = TL[:, u, 0:P]
                for c in range(0, w, 512):
                    n = min(512, w - c) // P
                    k0 = c // P * PAIR + h
                    keys = XX[:, k0:k0 + PAIR * (n - 1) + 1:PAIR, 0, :]
                    last = c + 512 >= w
                    mm(pS[u % 2][:, c:c + n * P], q, keys, start=True, stop=not last)
                mm(pS[u % 2][:, w - P:w], identb[:, :], maskb[:, :], start=False,
                   stop=True).then_inc(s_mm, 1)

            def projections(it, s):
                after(pe, xx_ev, it, XXN, min(s + XT_LEAD + 1, XXN))
                if s + XT_LEAD >= XXN:
                    after(pe, tl_ev, it, TLN, s + TV_LEAD)
                    if (s - 1 - RANK_LAG) % GRP == 0:
                        after(pe, place_rdy, it, NG, (s - 1 - RANK_LAG) // GRP + 1)
                u, v = s + TV_LEAD, s - L_LAG
                if is_tile(u):
                    mm(pM[:, 0:P], A_sb[:, :], XX[:, u, 0, :], start=True, stop=True)
                    i = mm(pM[:, P:2 * P], XX[:, u, 0, :], M_sb[:, :], start=True, stop=True)
                if is_tile(v):
                    i = mm(pM[:, 2 * P:2 * P + E], XX[:, v + X2T_LAG + XT_LEAD, 1, :], gwT[:, :],
                           start=True, stop=True)
                i.then_inc(tl_mm, 1)

            def turn(it, u):
                after(pe, p_rdy, it, NU, u + 1)
                for c in range(chunks(u + 1) - chunks(u)):
                    n = chunks(u) + c
                    after(pe, pt_ev, it, CHN, n - 1)
                    for kt in range(4 * c, min(4 * c + 4, u // PAIR + 1)):
                        i = nc.tensor.transpose(pT[n % 2][:, kt % 4 * P:(kt % 4 + 1) * P],
                                                Pr[:, u % 2, kt * P:(kt + 1) * P], identf[:, :])
                    i.then_inc(pt_mm, 1)

            def ranks(it, gr):
                after(pe, chosen_rdy, it, NG, gr + 1)
                after(pe, seen_rdy, it, NG, gr)
                after(pe, tl_ev, it, TLN, min(gr * GRP + RANK_LAG + TV_LEAD + 1, TLN))
                R = pM[:, 0:GRP * E].rearrange("p (a e) -> p a e", a=GRP)
                mm(R, onesb[:, :], seen[:, :].unsqueeze(1).to_broadcast([P, GRP, E]), start=True, stop=False)
                for a in range(GRP - 1):
                    mm(R[:, a + 1:, :], onesb[:, :],
                       chosen[:, a, :].unsqueeze(1).to_broadcast([P, GRP - 1 - a, E]), start=False, stop=False)
                mm(R, before[:, :], chosen[:, :, :], start=False, stop=True).then_inc(rank_mm, 1)

            def weigh(it, u):
                after(pe, pt_ev, it, CHN, chunks(u + 1))
                after(pe, x1_rdy, it, NU, u)
                for kt in range(u // PAIR + 1):
                    i = mm(pO[:, 0:D], PT[:, u % 2, kt * P:(kt + 1) * P], TL[:, kt * PAIR + u % PAIR, P:2 * P],
                           start=kt == 0, stop=kt == u // PAIR)
                i.then_inc(pv_mm, 1)

            with pe.Fori(0, ITERS) as it:
                for s in range(-XT_LEAD, NU + RANK_LAG):
                    if is_tile(s + XT_LEAD) or is_tile(s - X2T_LAG):
                        transposes(it, s)
                    if is_tile(s + S_LEAD):
                        scores(it, s + S_LEAD)
                    if is_tile(s + TV_LEAD) or is_tile(s - L_LAG):
                        projections(it, s)
                    if is_tile(s):
                        turn(it, s)
                    if s >= RANK_LAG and (s - RANK_LAG) % GRP == 0:
                        ranks(it, (s - RANK_LAG) // GRP)
                    if is_tile(s - PV_LAG):
                        weigh(it, s - PV_LAG)

            pe.wait_ge(seen_rdy, NG * ITERS + 1)
            pe.wait_ge(place_rdy, NG * ITERS + 1)
            mm(pM[:, 0:E], onesb[:, :], seen[:, :], start=True, stop=True).then_inc(cnt_mm, 1)
            pe.wait_ge(list_rdy, 1)
            pe.wait_ge(w_in, 48)

            def turn_x(m, j):
                t = m * LANES + j
                pe.wait_ge(xt_in[j], 16 * (m + 1))
                if not isinstance(t, int) or t >= 2:
                    pe.wait_ge(xT_rdy, t - 1)
                nc.tensor.transpose(bank[j % 2][:, 0:P], xt[:, j, 0:D], identf[:, :]).then_inc(xT_mm, 1)

            def up(m, j):
                t = m * LANES + j
                e = pe.value_load(eidx[0:1, ds(t, 1)], min_val=0, max_val=E - 1)
                pe.wait_ge(xT_rdy, t + 1)
                if not isinstance(t, int) or t >= 2:
                    pe.wait_ge(g_rdy, t - 1)
                mm(bank[2 + j % 2][:, :], xTs[:, j % 2, :], w13[:, ds(e, 1), :].rearrange("p o h -> p (o h)"),
                   start=True, stop=True).then_inc(h_mm, 1)

            def turn_g(m, j):
                t = m * LANES + j
                pe.wait_ge(g_rdy, t + 1)
                if not isinstance(t, int) or t >= 2:
                    pe.wait_ge(gT_rdy, t - 1)
                for c in range(H // P):
                    i = nc.tensor.transpose(bank[4 + j % 2][:, c * P:(c + 1) * P], g[:, j % 2, c * P:(c + 1) * P],
                                            identf[:, :])
                i.then_inc(gT_mm, 1)

            def down(m, j):
                t = m * LANES + j
                e = pe.value_load(eidx[0:1, ds(t, 1)], min_val=0, max_val=E - 1)
                pe.wait_ge(gT_rdy, t + 1)
                if not isinstance(t, int) or t >= 2:
                    pe.wait_ge(y_rdy, t - 1)
                for c in range(H // P):
                    i = mm(bank[6 + j % 2][:, 0:D], gTs[:, j % 2, c * P:(c + 1) * P],
                           w2_sb[:, ds(e, 1), c, :].rearrange("p o d -> p (o d)"),
                           start=c == 0, stop=c == H // P - 1)
                i.then_inc(y_mm, 1)

            def lane(m, j, lag):
                return m + (j - lag) // LANES, (j - lag) % LANES

            def step(m, j):
                first = isinstance(m, int) and m == 0
                if not isinstance(m, int) or m < NT // LANES:
                    up(m, j)
                if not first or j >= 1:
                    if not isinstance(m, int) or m * LANES + j <= NT:
                        turn_g(*lane(m, j, 1))
                if not isinstance(m, int) or m * LANES + j + 1 < NT:
                    turn_x(*lane(m, j, -1))
                if not first or j >= 2:
                    down(*lane(m, j, 2))

            turn_x(0, 0)
            for j in range(LANES):
                step(0, j)
            with pe.Fori(1, NT // LANES - 1) as m:
                for j in range(LANES):
                    step(m, j)
            for j in range(LANES):
                step(NT // LANES - 1, j)
            for j in range(2):
                step(NT // LANES, j)

        @block.scalar
        def _(act):
            copy = nc.scalar.activation
            act.wait_ge(A_mm, 1)
            copy(A_sb[:, :], pS[0][:, 0:P], ACT.Copy, scale=float(F_ATT) ** -0.5).then_inc(A_rdy, 1)

            def out_xx(it, s):
                q = s + XT_LEAD
                after(act, xx_mm, it, XXN, q + 1)
                lo, hi = 0 if is_tile(s + XT_LEAD) else 1, 2 if is_tile(s - X2T_LAG) else 1
                copy(XX[:, q, lo:hi, :], pM[:, lo * P:hi * P].rearrange("p (a b) -> p a b", b=P),
                     ACT.Copy).then_inc(xx_ev, 1)

            def out_tl(it, s):
                q = s + TV_LEAD
                after(act, tl_mm, it, TLN, q + 1)
                lo, hi = 0 if is_tile(s + TV_LEAD) else 2 * P, 2 * P + E if is_tile(s - L_LAG) else 2 * P
                copy(TL[:, q, lo:hi], pM[:, lo:hi], ACT.Copy).then_inc(tl_ev, 1)

            def out_pt(it, u):
                after(act, pv_mm, it, NU, u - 1)
                for c in range(chunks(u + 1) - chunks(u)):
                    n = chunks(u) + c
                    w = (min(4 * c + 4, u // PAIR + 1) - 4 * c) * P
                    after(act, pt_mm, it, CHN, n + 1)
                    copy(PT[:, u % 2, 4 * c * P:4 * c * P + w], pT[n % 2][:, 0:w], ACT.Copy).then_inc(pt_ev, 1)

            def exps(it, u):
                w = (u // PAIR + 1) * P
                after(act, max_rdy, it, NU, u + 1)
                after(act, pt_mm, it, CHN, chunks(u - 1) if u >= 1 else 0)
                after(act, rinv_rdy, it, NU, u - 3)
                sc = pS[u % 2][:, 0:w]
                copy(Pr[:, u % 2, 0:w], sc, ACT.Exp, bias=negmax[:, u % 4:u % 4 + 1], scale=1.0,
                     accum_out=rowsum[:, u % 4:u % 4 + 1]).then_inc(p_rdy, 1)

            def exp_logits(it, gr):
                after(act, dlog_rdy, it, NG, gr + 1)
                after(act, row_rdy, it, NG, gr)
                copy(elog[:, :, :], dlog[:, :, :], ACT.Exp).then_inc(elog_rdy, 1)

            with act.Fori(0, ITERS) as it:
                for s in range(-XT_LEAD, NU + PLACE_LAG):
                    if s == -XT_LEAD:
                        after(act, topi_rdy, it, NU, 0)
                    if is_tile(s + XT_LEAD) or is_tile(s - X2T_LAG):
                        out_xx(it, s)
                    if is_tile(s + TV_LEAD) or is_tile(s - L_LAG):
                        out_tl(it, s)
                    if is_tile(s):
                        out_pt(it, s)
                    if is_tile(s + S_LEAD):
                        exps(it, s + S_LEAD)
                    if s >= ROUTE_LAG and (s - ROUTE_LAG) % GRP == 0 and (s - ROUTE_LAG) // GRP < NG:
                        exp_logits(it, (s - ROUTE_LAG) // GRP)

            def silu(m, j):
                t = m * LANES + j
                act.wait_ge(h_mm, t + 1)
                if not isinstance(t, int) or t >= 2:
                    act.wait_ge(g_rdy, t - 1)
                nc.scalar.activation(sil[:, j % 2, :], bank[2 + j % 2][:, 0:H], ACT.Silu).then_inc(sil_rdy, 1)

            def out_g(m, j):
                t = m * LANES + j
                act.wait_ge(gT_mm, t + 1)
                if not isinstance(t, int) or t >= 2:
                    act.wait_ge(y_mm, t - 1)
                copy(gTs[:, j % 2, :], bank[4 + j % 2][:, 0:H], ACT.Copy).then_inc(gT_rdy, 1)

            silu(0, 0)
            for j in range(1, LANES):
                silu(0, j)
                out_g(0, j - 1)
            with act.Fori(1, NT // LANES) as m:
                for j in range(LANES):
                    silu(m, j)
                    out_g(m + (j - 1) // LANES, (j - 1) % LANES)
            out_g(NT // LANES - 1, LANES - 1)

        @block.vector
        def _(dve):
            v = nc.vector
            dve.wait_ge(consts, N_CONST)
            for c in range(2):
                dve.wait_ge(woT_mm, 4 * (c + 1))
                v.tensor_copy(woT[:, 4 * c:4 * c + 4, :].rearrange("p c q -> p (c q)"), pT[c][:, :]).then_inc(woT_rdy, 1)
            dve.wait_ge(gwT_mm, 1)
            v.tensor_copy(gwT[:, :], pO[:, 0:E]).then_inc(gwT_rdy, 1)
            dve.wait_ge(M_mm, 1)
            v.tensor_copy(M_sb[:, :], pS[1][:, 0:P]).then_inc(M_rdy, 1)

            def n_bn(s, kind):
                n = 0
                for z in range(-STAT1_LEAD, s + 1):
                    n += is_tile(z + STAT1_LEAD)
                    n += is_tile(z - X1_LAG) and (z < s or kind == 1)
                return n

            def X_tile(it, u):
                return X[:, ds(token_tile(it, u), 1), :].rearrange("p o d -> p (o d)")

            def maximum(it, u):
                w = (u // PAIR + 1) * P
                after(dve, s_mm, it, NU, u + 1)
                v.tensor_reduce(negmax[:, u % 4:u % 4 + 1], pS[u % 2][:, 0:w], AX.X, ALU.max,
                                negate=True).then_inc(max_rdy, 1)

            def attend(it, u):
                after(dve, rinv_rdy, it, NU, u + 1)
                after(dve, pv_mm, it, NU, u + 1)
                after(dve, xn_rdy, it, NU, min(u + STAT1_LEAD, NU))
                v.scalar_tensor_tensor(out=X_tile(it, u), in0=pO[:, 0:D], scalar=rinv[:, u % 4:u % 4 + 1],
                                       in1=X_tile(it, u), op0=ALU.mult, op1=ALU.add).then_inc(x1_rdy, 1)

            def stats(it, s, kind):
                u = s + STAT1_LEAD if kind == 0 else s - X1_LAG
                if kind == 0 and u == 0:
                    dve.wait_ge(x_in, it + 1)
                if kind == 0 and u == 2 * PAIR:
                    dve.wait_ge(x_mid, 32)
                if kind == 1:
                    after(dve, x1_rdy, it, NU, u + 1)
                after(dve, mv_rdy, it, STN, s - 2 + STAT1_LEAD + 1)
                alone(dve)
                v.bn_stats(bn[:, s % 2, kind, :], X_tile(it, u)).then_inc(bn_rdy, 1)

            def aggregate(it, s, kind, last):
                after(dve, bn_rdy, it, BNN, n_bn(s, kind))
                if kind == 0:
                    after(dve, xn_rdy, it, NU, s - 4 + STAT1_LEAD + 1)
                else:
                    after(dve, x2_rdy, it, NU, s - 4 - X1_LAG + 1)
                alone(dve)
                i = v.bn_aggr(mv[:, s % 4, kind, :], bn[:, s % 2, kind, :])
                if last:
                    i.then_inc(mv_rdy, 1)

            def norm1(it, s):
                u = s + NORM1_LEAD
                z = s - (STAT1_LEAD - NORM1_LEAD)
                after(dve, rstd_rdy, it, STN, z + STAT1_LEAD + 1)
                after(dve, xx_mm, it, XXN, u - 3)
                v.tensor_scalar(xn[:, u % 4, :], X_tile(it, u), mv[:, z % 4, 0, 0:1], rstd[:, z % 4, 0:1],
                                ALU.subtract, ALU.mult).then_inc(xn_rdy, 1)

            def norm2(it, s):
                u = s - NORM2_LAG
                z = s - (NORM2_LAG - X1_LAG)
                after(dve, rstd_rdy, it, STN, z + STAT1_LEAD + 1)
                if u == 0:
                    after(dve, rows_free, it, 1, 0)
                v.tensor_scalar(rows[:, u, :, 0:D],
                                X[:, ds(token_tile(it, u), 1), :].to_broadcast([P, K, D]),
                                mv[:, z % 4, 1, 0:1], rstd[:, z % 4, 1:2],
                                ALU.subtract, ALU.mult).then_inc(x2_rdy, 1)

            def top_values(it, u):
                after(dve, tl_ev, it, TLN, u + L_LAG + TV_LEAD + 1)
                if u % GRP == 0:
                    after(dve, hot_rdy, it, NG, u // GRP - 1)
                alone(dve)
                v.max(top[:, u // GRP % 2, u % GRP, :], TL[:, u + L_LAG + TV_LEAD, 2 * P:]).then_inc(top_rdy, 1)

            def top_experts(it, u):
                after(dve, top_rdy, it, NU, u + 1)
                alone(dve)
                v.max_index(topi[:, u // GRP % 2, u % GRP, :], top[:, u // GRP % 2, u % GRP, :],
                            TL[:, u + L_LAG + TV_LEAD, 2 * P:]).then_inc(topi_rdy, 1)

            def route(it, gr):
                z = gr % 2
                after(dve, topi_rdy, it, NU, GRP * (gr + 1))
                after(dve, rank_mm, it, NG, gr)
                after(dve, row_rdy, it, NG, gr)
                after(dve, elog_rdy, it, NG, gr)
                v.tensor_tensor(dlog[:, :, :], top[:, z, :, :], top[:, z, :, 0:1].to_broadcast([P, GRP, 8]),
                                ALU.subtract).then_inc(dlog_rdy, 1)
                v.tensor_tensor(hot[:, :, :, :], topi[:, z, :, 0:K].unsqueeze(3).to_broadcast([P, GRP, K, E]),
                                iota8[:, :].unsqueeze(1).unsqueeze(1).to_broadcast([P, GRP, K, E]),
                                ALU.is_equal).then_inc(hot_rdy, 1)
                after(dve, hot_rdy, it, NG, gr + 1)
                v.tensor_tensor(chosen[:, :, :], hot[:, :, 0, :], hot[:, :, 1, :], ALU.add).then_inc(chosen_rdy, 1)
                after(dve, chosen_rdy, it, NG, gr + 1)
                with nc.allow_low_precision("counts of at most 4"):
                    v.tensor_reduce(newc[:, :], chosen[:, :, :].rearrange("p a e -> p e a"), AX.X,
                                    ALU.add).then_inc(newc_rdy, 1)

            def places(it, gr):
                after(dve, rank_mm, it, NG, gr + 1)
                v.tensor_tensor(place[:, :, :], pM[:, 0:GRP * E].rearrange("p (a e) -> p a e", a=GRP),
                                stretch0[:, :].unsqueeze(1).to_broadcast([P, GRP, E]),
                                ALU.add).then_inc(place_rdy, 1)

            def place_rows(it, gr):
                a0 = gr * GRP
                after(dve, newc_rdy, it, NG, gr + 1)
                v.tensor_tensor(seen[:, :], seen[:, :], newc[:, :], ALU.add).then_inc(seen_rdy, 1)
                after(dve, elog_rdy, it, NG, gr + 1)
                v.tensor_reduce(esum[:, :], elog[:, :, :], AX.X, ALU.add).then_inc(esum_rdy, 1)
                after(dve, place_rdy, it, NG, gr + 1)
                v.tensor_tensor(picked[:, :, :, :], hot[:, :, :, :],
                                place[:, :, :].unsqueeze(2).to_broadcast([P, GRP, K, E]),
                                ALU.mult).then_inc(picked_rdy, 1)
                after(dve, esum_rdy, it, NG, gr + 1)
                v.reciprocal(einv[:, :], esum[:, :]).then_inc(einv_rdy, 1)
                for h in range(PAIR):
                    v.tensor_copy(rows[:, a0 + h:a0 + GRP:PAIR, :, COL_DEST].bitcast(u32),
                                  dests[:, ds(it, 1), h, a0 // PAIR:(a0 + GRP) // PAIR, :]
                                  .rearrange("p o i k -> p (o i) k").bitcast(u32))
                after(dve, picked_rdy, it, NG, gr + 1)
                with nc.allow_low_precision("row numbers, exact in float32"):
                    v.tensor_reduce(slots[:, a0:a0 + GRP, :], picked[:, :, :, :], AX.X, ALU.add)
                after(dve, einv_rdy, it, NG, gr + 1)
                v.tensor_tensor(rows[:, a0:a0 + GRP, :, COL_W], elog[:, :, 0:K],
                                einv[:, :].unsqueeze(2).to_broadcast([P, GRP, K]), ALU.mult).then_inc(row_rdy, 1)

            with dve.Fori(0, ITERS) as it:
                for s in range(-STAT1_LEAD, NU + PLACE_LAG):
                    ln1, ln2 = is_tile(s + STAT1_LEAD), is_tile(s - X1_LAG)
                    if s >= PLACE_LAG and (s - PLACE_LAG) % GRP == 0:
                        places(it, (s - PLACE_LAG) // GRP)
                    if ln2:
                        u = s - X1_LAG
                        after(dve, p_rdy, it, NU, u + 1)
                        v.reciprocal(rinv[:, u % 4:u % 4 + 1], rowsum[:, u % 4:u % 4 + 1]).then_inc(rinv_rdy, 1)
                    if ln1:
                        stats(it, s, 0)
                    if ln2:
                        attend(it, s - X1_LAG)
                    if ln1:
                        aggregate(it, s, 0, not ln2)
                    if ln2:
                        stats(it, s, 1)
                    if is_tile(s + S_LEAD):
                        maximum(it, s + S_LEAD)
                    if ln2:
                        aggregate(it, s, 1, True)
                    if is_tile(s + NORM1_LEAD):
                        norm1(it, s)
                    if is_tile(s - TOP_LAG):
                        top_values(it, s - TOP_LAG)
                    if is_tile(s - NORM2_LAG):
                        norm2(it, s)
                    if is_tile(s - TOP_LAG):
                        top_experts(it, s - TOP_LAG)
                    if s >= ROUTE_LAG and (s - ROUTE_LAG) % GRP == 0 and (s - ROUTE_LAG) // GRP < NG:
                        route(it, (s - ROUTE_LAG) // GRP)
                    if s >= PLACE_LAG and (s - PLACE_LAG) % GRP == 0:
                        place_rows(it, (s - PLACE_LAG) // GRP)

            n_link = [0]

            def link(i):
                n_link[0] += 1
                i.then_inc(listing, 1)
                dve.wait_ge(listing, n_link[0])

            dve.wait_ge(cnt_mm, 1)
            link(v.tensor_copy(cnt[:, :], pM[0:1, 0:E]))
            link(v.tensor_scalar(cnti[:, :], cnt[:, :], float(P - 1), None, ALU.add))
            link(v.tensor_scalar(nti[:, :], cnti[:, :], P.bit_length() - 1, None, ALU.logical_shift_right))
            link(v.tensor_copy(ntf[:, :], nti[:, :]))
            link(v.tensor_tensor_scan(ntcum[:, :], ntf[:, :], zero8[:, :], 0.0, ALU.add, ALU.add))
            link(v.tensor_tensor(pad0[:, :], cnt[:, :], stretch0[0:1, :], ALU.add))
            link(v.tensor_tensor(past[:, :, :], ntcum[:, :].unsqueeze(1).to_broadcast([1, NT, E]),
                                 iotat[:, :].unsqueeze(2).to_broadcast([1, NT, E]), ALU.is_le))
            link(v.tensor_reduce(e_of[:, :], past[:, :, :], AX.X, ALU.add))
            link(v.tensor_tensor(pastn[:, :, :], past[:, :, :], ntf[:, :].unsqueeze(1).to_broadcast([1, NT, E]), ALU.mult))
            link(v.tensor_reduce(s_of[:, :], pastn[:, :, :], AX.X, ALU.add))
            link(v.tensor_tensor(s_of[:, :], iotat[:, :], s_of[:, :], ALU.subtract))
            link(v.tensor_scalar(r_of[:, :], s_of[:, :], float(P), None, ALU.mult))
            link(v.scalar_tensor_tensor(out=row0[:, :], in0=e_of[:, :], scalar=float(STRETCH), in1=r_of[:, :],
                                        op0=ALU.mult, op1=ALU.add))
            v.tensor_scalar(eidx[:, :], e_of[:, :], float(E - 1), None, ALU.min).then_inc(list_rdy, 1)

            def out_x(m, j):
                t = m * LANES + j
                dve.wait_ge(xT_mm, t + 1)
                if not isinstance(t, int) or t >= 2:
                    dve.wait_ge(h_mm, t - 1)
                v.tensor_copy(xTs[:, j % 2, :], bank[j % 2][:, 0:P]).then_inc(xT_rdy, 1)

            def gated(m, j):
                t = m * LANES + j
                dve.wait_ge(sil_rdy, t + 1)
                if not isinstance(t, int) or t >= 2:
                    dve.wait_ge(gT_mm, t - 1)
                v.tensor_tensor(g[:, j % 2, :], sil[:, j % 2, :], bank[2 + j % 2][:, H:2 * H],
                                ALU.mult).then_inc(g_rdy, 1)

            def weighted(m, j):
                t = m * LANES + j
                if not isinstance(m, int) or m >= 1:
                    dve.wait_ge(y_out[j], 16 * m)
                v.tensor_copy(ydest[:, j:j + 1], xt[:, j, COL_DEST:COL_DEST + 1].bitcast(u32))
                dve.wait_ge(y_mm, t + 1)
                v.tensor_scalar(ysb[:, j, :], bank[6 + j % 2][:, 0:D], xt[:, j, COL_W:COL_W + 1], None,
                                ALU.mult).then_inc(y_rdy, 1)

            def step(m, j):
                static = isinstance(m, int)
                if not static or m * LANES + j + 1 < NT:
                    out_x(m + (j + 1) // LANES, (j + 1) % LANES)
                if not static or m < NT // LANES:
                    gated(m, j)
                if not static or m * LANES + j >= 2:
                    weighted(m + (j - 2) // LANES, (j - 2) % LANES)

            out_x(0, 0)
            for m in range(2):
                for j in range(LANES):
                    step(m, j)
            with dve.Fori(2, NT // LANES - 1) as m:
                for j in range(LANES):
                    step(m, j)
            for j in range(LANES):
                step(NT // LANES - 1, j)
            for j in range(2):
                step(NT // LANES, j)

            for c in range(NF):
                Xc = X[:, c * FIN:(c + 1) * FIN, :]
                dve.wait_ge(yf_in[c % 2], 32 * (c // 2 + 1))
                v.tensor_tensor(Xc, Xc, yf[:, c % 2, 0, :, :], ALU.add).then_inc(sum0, 1)
                dve.wait_ge(sum0, c + 1)
                v.tensor_tensor(Xc, Xc, yf[:, c % 2, 1, :, :], ALU.add).then_inc(sum1, 1)


_INS = ["L0_attn_in_features", "L0_attn_w_q", "L0_attn_w_k", "L0_attn_w_v", "L0_attn_w_o",
        "L0_ffn_gate_w", "L0_ffn_w1", "L0_ffn_w2", "L0_ffn_w3"]
_OUT = (B, S, D)


def kernel(**inputs):
    import concourse.bacc as bacc
    from concourse.bass_utils import run_bass_kernel_spmd

    nc = bacc.Bacc("TRN2", target_bir_lowering=False, num_devices=1)
    arrays, args = {}, []
    for name in _INS:
        a = np.ascontiguousarray(inputs[name])
        arrays[name] = a
        args.append(nc.dram_tensor(name, a.shape, mybir.dt.from_np(a.dtype), kind="ExternalInput").ap())
    out = nc.dram_tensor("out", _OUT, mybir.dt.float32, kind="ExternalOutput").ap()
    build(nc, *args, out)
    result = run_bass_kernel_spmd(nc, [arrays], core_ids=[0])
    return result.results[0]["out"]
```

```python
from contextlib import ExitStack

import numpy as np

import concourse.bass as bass
from concourse import mybir

P = 128
B, S, D = 4, 1024, 128
E, H, K = 8, 256, 2
F_ATT = 1024
EPS = 1e-5
N_TOK = B * S
QT = S // P
PAIR = 2
NU = PAIR * QT
N_TILES = B * QT
FC = F_ATT // P
GROUPS = [(a, 4) for a in range(0, N_TILES - 4, 4)] + [(N_TILES - 4, 2), (N_TILES - 2, 2)]
NG = len(GROUPS)
ROWS_RING = 16
GROUPS_OF = {a + n: gr for gr, (a, n) in enumerate(GROUPS) for n in range(GROUPS[gr][1])}
ROW = D + 4
COL_DEST, COL_W = D, D + 1
STRETCH = N_TOK + P
LANES = 8
MOST_TILES = (K * N_TOK + E * (P - 1)) // P
NT = -(-MOST_TILES // LANES) * LANES
SPARE = NT - K * N_TOK // P
XS_ROWS = E * STRETCH + SPARE * P
YB_ROWS = K * N_TOK + (E + SPARE) * P
MASK = -3.0e38
IN_RANGE = "counts add up to K * N_TOK, and the expert number of a list entry is clamped to E - 1"
WIDE = 2 * H + H // P * D
LIST0 = 4

XT_LEAD, TV_LEAD, S_LEAD = 3, 2, 1
STAT1_LEAD, NORM1_LEAD, STAT1_GROUP = 9, 4, 4
PV_LAG, X1_LAG, NORM2_LAG, X2T_LAG, L_LAG, TOP_LAG = 1, 2, 3, 4, 5, 6
ROUTE_LAG, RANK_LAG, PLACE_LAG = 6, 7, 8


def build(nc, x, w_q, w_k, w_v, w_o, gate_w, w1, w2, w3, out):
    f32, bf16 = mybir.dt.float32, mybir.dt.bfloat16
    i32, u32 = mybir.dt.int32, mybir.dt.uint32
    ALU, ACT, AX = mybir.AluOpType, mybir.ActivationFunctionType, mybir.AxisListType
    ds = bass.ds

    xs = nc.dram_tensor("expert_rows", (XS_ROWS, ROW), f32, kind="Internal").ap()
    yb = nc.dram_tensor("choice_rows", (YB_ROWS, D), f32, kind="Internal").ap()

    ctx = ExitStack()
    with ctx:
        def sb(name, shape, dt=f32):
            return ctx.enter_context(nc.sbuf_tensor(name, shape, dt))

        def pb(name):
            return ctx.enter_context(nc.psum_tensor(name, [P, 512], f32))

        def sem(name):
            return ctx.enter_context(nc.semaphore(name))

        X = sb("X", [P, N_TILES, D])
        WB = sb("WB", [P, E * WIDE])
        WE = WB[:, :].rearrange("p (e h) -> p e h", e=E)
        wq_sb, wk_sb, wo_sb, wv_sb = (WB[:, n * F_ATT:(n + 1) * F_ATT] for n in range(4))
        wq_sb, wk_sb, wv_sb = (w.rearrange("p (c d) -> p c d", c=FC) for w in (wq_sb, wk_sb, wv_sb))
        woT = sb("woT", [P, FC, P])
        A_sb, M_sb = sb("A_sb", [P, P]), sb("M_sb", [P, P])
        gw_sb, gwT = sb("gw_sb", [E, D]), sb("gwT", [P, E])
        identf, identb = sb("identf", [P, P]), sb("identb", [P, P], bf16)
        maskb = sb("maskb", [P, P], bf16)
        before = sb("before", [P, P], bf16)
        onesb = sb("onesb", [P, P], bf16)
        halves = sb("halves", [P, STAT1_GROUP])
        iota8 = sb("iota8", [P, E])
        stretch0 = sb("stretch0", [P, E])
        dests = sb("dests", [P, B // PAIR, PAIR, QT, K])
        xn = sb("xn", [P, 4, D])
        XX = sb("XX", [P, N_TILES + 4, P])
        TL = sb("TL", [P, N_TILES + L_LAG + TV_LEAD, 2 * P + E])
        Pr = sb("Pr", [P, 2, S])
        PT = sb("PT", [P, 2, S])
        negmax, rowsum, rinv = (sb(n, [P, N_TILES]) for n in ("negmax", "rowsum", "rinv"))
        bn1, bn2 = sb("bn1", [P, N_TILES, 6]), sb("bn2", [P, N_TILES, 6])
        mv1, mv2 = sb("mv1", [P, N_TILES, 2]), sb("mv2", [P, N_TILES, 2])
        ve1, ve2 = sb("ve1", [P, N_TILES]), sb("ve2", [P, N_TILES])
        rstd1, rstd2 = sb("rstd1", [P, N_TILES]), sb("rstd2", [P, N_TILES])
        rows = sb("rows", [P, ROWS_RING, K, ROW])
        top, topi = sb("top", [P, N_TILES, 8]), sb("topi", [P, N_TILES, 8], u32)
        dlog, elog = sb("dlog", [P, N_TILES, 8]), sb("elog", [P, N_TILES, 8])
        esum, einv = sb("esum", [P, N_TILES]), sb("einv", [P, N_TILES])
        hot = sb("hot", [P, N_TILES, K, E], bf16)
        chosen = sb("chosen", [P, N_TILES, E], bf16)
        newc, seen = sb("newc", [P, NG, E], bf16), sb("seen", [P, NG + 1, E], bf16)
        place = sb("place", [P, N_TILES, E])
        picked = sb("picked", [P, 2, 4, K, E])
        slots = sb("slots", [P, N_TILES, K], u32)
        cnt, cnti = sb("cnt", [1, E]), sb("cnti", [1, E], i32)
        nti, ntf, zero8, ntcum = sb("nti", [1, E], i32), sb("ntf", [1, E]), sb("zero8", [1, E]), sb("ntcum", [1, E])
        pad0 = sb("pad0", [1, E], i32)
        iotat = sb("iotat", [1, NT])
        past, pastn = sb("past", [1, NT, E]), sb("pastn", [1, NT, E])
        e_of, s_of, i_of, r_of = (sb(n, [1, NT]) for n in ("e_of", "s_of", "i_of", "r_of"))
        row0, wcol = sb("row0", [1, NT], i32), sb("wcol", [1, LIST0 + NT], i32)
        padrows = sb("padrows", [P, E + SPARE, ROW])
        xt = sb("xt", [P, LANES, ROW])
        xTs = sb("xTs", [P, 2, P])
        sil, g = sb("sil", [P, 2, H]), sb("g", [P, 2, H])
        gTs = sb("gTs", [P, 2, H])
        ysb, ydest = sb("ysb", [P, LANES, D]), sb("ydest", [P, LANES], u32)
        FIN = 4
        NF = N_TILES // FIN
        ZF = 4
        yf = XX[:, 0:ZF * K * FIN, :].rearrange("p (z k i) d -> p z k i d", z=ZF, k=K)

        pS = [ctx.enter_context(nc.psum_tensor(f"scores{i}", [P, 1024], f32)) for i in range(2)]
        pT, (pM, pO) = [pb("turned0"), pb("turned1")], [pb("mixed"), pb("weighed")]
        bank = [pS[0][:, 0:512], pS[0][:, 512:], pS[1][:, 0:512], pS[1][:, 512:], *pT, pM, pO]

        x_head, x_mid, x_tail = sem("x_head"), sem("x_mid"), sem("x_tail")
        wqk_in, wv_in, wo_in, gw_in, w_in = sem("wqk_in"), sem("wv_in"), sem("wo_in"), sem("gw_in"), sem("w_in")
        const0, ident_rdy, consts, pads_rdy = sem("const0"), sem("ident_rdy"), sem("consts"), sem("pads_rdy")
        A_mm, woT_mm, M_mm, gwT_mm = sem("A_mm"), sem("woT_mm"), sem("M_mm"), sem("gwT_mm")
        A_rdy, woT_rdy, M_rdy, gwT_rdy = sem("A_rdy"), sem("woT_rdy"), sem("M_rdy"), sem("gwT_rdy")
        bn1_rdy, mv1_rdy, ve1_rdy, rstd1_rdy = sem("bn1_rdy"), sem("mv1_rdy"), sem("ve1_rdy"), sem("rstd1_rdy")
        bn2_rdy, mv2_rdy, ve2_rdy, rstd2_rdy = sem("bn2_rdy"), sem("mv2_rdy"), sem("ve2_rdy"), sem("rstd2_rdy")
        xn_rdy, xx_mm, xx_ev, tl_mm, tl_ev = sem("xn_rdy"), sem("xx_mm"), sem("xx_ev"), sem("tl_mm"), sem("tl_ev")
        s_mm, max_rdy, p_rdy = sem("s_mm"), sem("max_rdy"), sem("p_rdy")
        pt_mm, pt_ev, pv_mm, rinv_rdy, x1_rdy = sem("pt_mm"), sem("pt_ev"), sem("pv_mm"), sem("rinv_rdy"), sem("x1_rdy")
        x2_rdy, top_rdy, topi_rdy = sem("x2_rdy"), sem("top_rdy"), sem("topi_rdy")
        dlog_rdy, elog_rdy, hot_rdy, chosen_rdy = sem("dlog_rdy"), sem("elog_rdy"), sem("hot_rdy"), sem("chosen_rdy")
        newc_rdy, seen_rdy, rank_mm, place_rdy, picked_rdy = sem("newc_rdy"), sem("seen_rdy"), sem("rank_mm"), sem("place_rdy"), sem("picked_rdy")
        esum_rdy, einv_rdy, row_rdy = sem("esum_rdy"), sem("einv_rdy"), sem("row_rdy")
        scattered = [sem(f"scattered{gr}") for gr in range(NG)]
        held = sem("held")
        cnt_mm, listing, list_rdy, padded = sem("cnt_mm"), sem("listing"), sem("list_rdy"), sem("padded")
        xt_in = [sem(f"xt_in{j}") for j in range(LANES)]
        y_out = [sem(f"y_out{j}") for j in range(LANES)]
        xT_mm, xT_rdy, h_mm, sil_rdy, g_rdy = sem("xT_mm"), sem("xT_rdy"), sem("h_mm"), sem("sil_rdy"), sem("g_rdy")
        gT_mm, gT_rdy, y_mm, y_rdy = sem("gT_mm"), sem("gT_rdy"), sem("y_mm"), sem("y_rdy")
        yf_in = [sem(f"yf_in{j}") for j in range(ZF)]
        sum0, sum1, out_done = sem("sum0"), sem("sum1"), sem("out_done")
        N_CONST, N_PADS, M_TILES = 6 + K, 8, NT // LANES

        def is_tile(u):
            return 0 <= u < N_TILES

        def blocks(u):
            return u % NU // PAIR + 1

        def keys_of(u):
            return u // NU * NU + u % PAIR, u

        def chunks(u):
            return sum(-(-blocks(v) // 4) for v in range(u))

        def token_tile(u):
            return u // NU * NU + (u % PAIR) * QT + u % NU // PAIR

        def group_at(s, lag):
            return next((gr for gr, (a, n) in enumerate(GROUPS) if a + n - 1 + lag == s), None)

        def wait(eng, semaphore, count):
            if count > 0:
                eng.wait_ge(semaphore, count)

        def has_xx(s):
            return is_tile(s + XT_LEAD) or is_tile(s - X2T_LAG)

        def has_tl(s):
            return is_tile(s + TV_LEAD) or is_tile(s - L_LAG)

        def n_xx(s):
            return sum(has_xx(z) for z in range(-XT_LEAD, s + 1))

        def n_tl(s):
            return sum(has_tl(z) for z in range(-TV_LEAD, s + 1))

        LAST_SLOT = N_TILES - 1 + PLACE_LAG
        block = ctx.enter_context(nc.Block())

        def pad(eng, experts):
            eng.wait_ge(pads_rdy, N_PADS)
            eng.wait_ge(list_rdy, 1)
            _, starts = nc.values_load_multi_w_load_instructions(
                pad0[0:1, experts[0]:experts[-1] + 1], engines=[eng.engine], min_val=0, max_val=XS_ROWS - P,
                skip_runtime_bounds_check_because=IN_RANGE)
            for e, r in zip(experts, starts):
                eng.dma_start(xs[ds(r, P), :], padrows[:, e, :]).then_inc(padded, 16)

        @block.sync
        def _(sp):
            xv = x.rearrange("b (i p) d -> p b i d", p=P)
            Xv = X[:, :, :].rearrange("p (b i) d -> p b i d", b=B)
            for b in range(PAIR):
                sp.dma_start(Xv[:, b, 0:2, :], xv[:, b, 0:2, :]).then_inc(x_head, 16)
            sp.dma_start(wq_sb, w_q.rearrange("(p c) i -> p c i", p=P)).then_inc(wqk_in, 16)
            sp.dma_start(wk_sb, w_k.rearrange("(p c) i -> p c i", p=P)).then_inc(wqk_in, 16)
            sp.dma_start(wo_sb, w_o).then_inc(wo_in, 16)
            sp.dma_start(wv_sb, w_v.rearrange("(p c) i -> p c i", p=P)).then_inc(wv_in, 16)
            sp.dma_start(gw_sb[:, :], gate_w).then_inc(gw_in, 16)
            for b in range(PAIR):
                sp.dma_start(Xv[:, b, 2:QT, :], xv[:, b, 2:QT, :]).then_inc(x_mid, 16)
            for b in range(PAIR, B):
                sp.dma_start(Xv[:, b, :, :], xv[:, b, :, :]).then_inc(x_tail, 16)
            sp.wait_ge(A_mm, 1)
            sp.wait_ge(M_mm, 1)
            sp.dma_start(WE[:, :, 0:H], w1.rearrange("e p h -> p e h")).then_inc(w_in, 16)
            sp.dma_start(WE[:, :, H:2 * H], w3.rearrange("e p h -> p e h")).then_inc(w_in, 16)
            for c in range(H // P):
                sp.dma_start(WE[:, :, 2 * H + c * D:2 * H + (c + 1) * D],
                             w2.rearrange("e (t p) d -> p t e d", p=P)[:, c]).then_inc(w_in, 16)
            sp.wait_ge(pads_rdy, N_PADS)
            sp.dma_start(xs[E * STRETCH:XS_ROWS, :].rearrange("(j p) c -> p j c", p=P),
                         padrows[:, E:, :]).then_inc(padded, 16)
            pad(sp, range(E // 2))
            for gr in range(NG):
                sp.wait_ge(scattered[gr], 16 * K * GROUPS[gr][1])
            sp.wait_ge(padded, 16 * (E + 1))
            sp.wait_ge(list_rdy, 2)

            def load(m):
                _, firsts = nc.values_load_multi_w_load_instructions(
                    row0[0:1, ds(m * LANES, LANES)], engines=[sp.engine], min_val=0, max_val=XS_ROWS - P,
                    skip_runtime_bounds_check_because=IN_RANGE)
                for j, r in enumerate(firsts):
                    if not isinstance(m, int):
                        sp.wait_ge(y_rdy, m * LANES + j - LANES + 1)
                    sp.dma_start(xt[:, j, :], xs[ds(r, P), :]).then_inc(xt_in[j], 16)

            load(0)
            with sp.Fori(1, M_TILES) as m:
                load(m)

            for j in range(LANES):
                sp.wait_ge(y_out[j], 16 * M_TILES)
            yv = yb[0:K * N_TOK, :].rearrange("(k c i p) d -> p k c i d", k=K, c=NF, i=FIN)
            ov = out.rearrange("b (c i p) d -> (b c) p i d", c=NF // B, i=FIN)

            def fetch(c):
                for k in range(K):
                    sp.dma_start(yf[:, c % ZF, k, :, :], yv[:, k, c, :, :]).then_inc(yf_in[c % ZF], 16)

            for c in range(ZF):
                fetch(c)
            for c in range(NF):
                sp.wait_ge(sum1, c + 1)
                sp.dma_start(ov[c], X[:, c * FIN:(c + 1) * FIN, :]).then_inc(out_done, 16)
                if c + ZF < NF:
                    fetch(c + ZF)
            sp.wait_ge(out_done, 16 * NF)

        @block.gpsimd
        def _(pool):
            nc.gpsimd.memset(identf[:, :], 0.0).then_inc(const0, 1)
            pool.wait_ge(const0, 1)
            nc.gpsimd.affine_select(out=identf[:, :], in_=identf[:, :], compare_op=ALU.not_equal, fill=1.0,
                                    base=0, pattern=[[-1, P]], channel_multiplier=1).then_inc(ident_rdy, 1)
            nc.gpsimd.memset(halves[:, :], -0.5).then_inc(consts, 1)

            def rstd_1(u0):
                t = slice(u0, u0 + STAT1_GROUP)
                pool.wait_ge(mv1_rdy, u0 + STAT1_GROUP)
                nc.gpsimd.tensor_scalar_add(ve1[:, t], mv1[:, t, 1], EPS).then_inc(ve1_rdy, 1)
                pool.wait_ge(ve1_rdy, u0 // STAT1_GROUP + 1)
                nc.gpsimd.tensor_tensor(rstd1[:, t], ve1[:, t], halves[:, :], ALU.pow).then_inc(rstd1_rdy, 1)

            def rstd_2(u):
                pool.wait_ge(mv2_rdy, u + 1)
                nc.gpsimd.tensor_scalar_add(ve2[:, u:u + 1], mv2[:, u, 1:2], EPS).then_inc(ve2_rdy, 1)
                pool.wait_ge(ve2_rdy, u + 1)
                nc.gpsimd.tensor_tensor(rstd2[:, u:u + 1], ve2[:, u:u + 1], halves[:, 0:1],
                                        ALU.pow).then_inc(rstd2_rdy, 1)

            def more_constants():
                nc.gpsimd.memset(maskb[:, :], 0.0).then_inc(const0, 1)
                nc.gpsimd.memset(onesb[:, :], 1.0).then_inc(consts, 1)
                pool.wait_ge(const0, 2)
                pool.wait_ge(consts, 2)
                nc.gpsimd.affine_select(out=maskb[:, :], in_=maskb[:, :], compare_op=ALU.is_ge, fill=MASK,
                                        base=0, pattern=[[-1, P]], channel_multiplier=1).then_inc(consts, 1)
                nc.gpsimd.tensor_copy(identb[:, :], identf[:, :]).then_inc(consts, 1)
                nc.gpsimd.affine_select(out=before[:, :], in_=onesb[:, :], compare_op=ALU.is_gt, fill=0.0,
                                        base=0, pattern=[[1, P]], channel_multiplier=-1).then_inc(consts, 1)
                nc.gpsimd.memset(seen[:, 0, :], 0.0).then_inc(consts, 1)
                for k in range(K):
                    nc.gpsimd.iota(dests[:, :, :, :, k].bitcast(u32), [[NU * P, B // PAIR], [S, PAIR], [P, QT]],
                                   base=k * N_TOK, channel_multiplier=1).then_inc(consts, 1)
                nc.gpsimd.iota(iota8[:, :], [[1, E]], base=0, channel_multiplier=0,
                               allow_small_or_imprecise_dtypes=True).then_inc(pads_rdy, 1)
                nc.gpsimd.iota(stretch0[:, :], [[STRETCH, E]], base=0, channel_multiplier=0,
                               allow_small_or_imprecise_dtypes=True).then_inc(pads_rdy, 1)
                nc.gpsimd.iota(iotat[:, :], [[1, NT]], base=0, channel_multiplier=0,
                               allow_small_or_imprecise_dtypes=True).then_inc(pads_rdy, 1)
                nc.gpsimd.memset(zero8[:, :], 0.0).then_inc(pads_rdy, 1)
                nc.gpsimd.memset(wcol[:, 0:LIST0].bitcast(f32), 0.0).then_inc(pads_rdy, 1)
                nc.gpsimd.memset(rows[:, :, :, D:ROW], 0.0).then_inc(pads_rdy, 1)
                nc.gpsimd.memset(padrows[:, :, :], 0.0).then_inc(pads_rdy, 1)
                pool.wait_ge(pads_rdy, 7)
                nc.gpsimd.iota(padrows[:, :, COL_DEST].bitcast(u32), [[P, E + SPARE]], base=K * N_TOK,
                               channel_multiplier=1).then_inc(pads_rdy, 1)

            def scatter(gr, u, k):
                if (u, k) == (GROUPS[gr][0], 0):
                    pool.wait_ge(row_rdy, gr + 1)
                nc.gpsimd.indirect_dma_start(
                    xs, bass.IndirectOffsetOnAxis(ap=slots[:, u, k:k + 1], axis=0),
                    rows[:, u % ROWS_RING, k, :], None).then_inc(scattered[gr], 16)

            waiting, room = [], 0.0
            for s in range(-STAT1_LEAD, LAST_SLOT + 1):
                u = s + STAT1_LEAD
                if is_tile(u) and u % STAT1_GROUP == STAT1_GROUP - 1:
                    rstd_1(u - STAT1_GROUP + 1)
                if u == STAT1_GROUP - 1:
                    more_constants()
                if is_tile(s - X1_LAG):
                    rstd_2(s - X1_LAG)
                gr = group_at(s, PLACE_LAG)
                if gr is not None:
                    a, n = GROUPS[gr]
                    waiting += [(gr, v, k) for v in range(a, a + n) for k in range(K)]
                room = min(room + (0.55 * blocks(s) + 0.3 if is_tile(s) else 0.0), 2.0)
                while waiting and room >= 1:
                    scatter(*waiting.pop(0))
                    room -= 1
            for item in waiting:
                scatter(*item)

            def store(m, j):
                pool.wait_ge(y_rdy, m * LANES + j + 1)
                pool.sem_inc(held, 1)
                nc.gpsimd.indirect_dma_start(
                    yb, bass.IndirectOffsetOnAxis(ap=ydest[:, j:j + 1], axis=0),
                    ysb[:, j, :], None).then_inc(y_out[j], 16)

            with pool.Fori(0, M_TILES) as m:
                for j in range(LANES):
                    store(m, j)

        @block.tensor
        def _(pe):
            mm = nc.tensor.matmul

            def transposes(s):
                if has_tl(s - 1):
                    pe.wait_ge(tl_ev, n_tl(s - 1))
                else:
                    wait(pe, xx_ev, n_xx(s - 1))
                gr = group_at(s - 1, RANK_LAG)
                if gr is not None:
                    pe.wait_ge(place_rdy, gr + 1)
                u, v = s + XT_LEAD, s - X2T_LAG
                if is_tile(u):
                    pe.wait_ge(xn_rdy, u + 1)
                    i = nc.tensor.transpose(pM[:, 0:P], xn[:, u % 4, :], identf[:, :])
                if is_tile(v):
                    pe.wait_ge(x2_rdy, v + 1)
                    i = nc.tensor.transpose(pM[:, P:2 * P], rows[:, v % ROWS_RING, 0, 0:D], identf[:, :])
                i.then_inc(xx_mm, 1)

            def scores(u):
                pe.wait_ge(tl_ev, n_tl(u - TV_LEAD))
                k0, w = keys_of(u)[0], blocks(u) * P
                for c in range(0, w, 512):
                    n = min(512, w - c) // P
                    first = k0 + PAIR * (c // P)
                    keys = XX[:, first:first + PAIR * (n - 1) + 1:PAIR, :]
                    mm(pS[u % 2][:, c:c + n * P], TL[:, u, 0:P], keys, start=True, stop=c + 512 < w)
                mm(pS[u % 2][:, w - P:w], identb[:, :], maskb[:, :], start=False, stop=True).then_inc(s_mm, 1)

            def projections(s):
                pe.wait_ge(xx_ev, n_xx(s))
                if not has_xx(s):
                    wait(pe, tl_ev, n_tl(s - 1))
                    gr = group_at(s - 1, RANK_LAG)
                    if gr is not None:
                        pe.wait_ge(place_rdy, gr + 1)
                u, v = s + TV_LEAD, s - L_LAG
                if is_tile(u):
                    mm(pM[:, 0:P], A_sb[:, :], XX[:, u, :], start=True, stop=True)
                    i = mm(pM[:, P:2 * P], XX[:, u, :], M_sb[:, :], start=True, stop=True)
                if is_tile(v):
                    i = mm(pM[:, 2 * P:2 * P + E], XX[:, N_TILES + v % 4, :], gwT[:, :], start=True, stop=True)
                i.then_inc(tl_mm, 1)

            def turn(u):
                pe.wait_ge(p_rdy, u + 1)
                for c in range(chunks(u + 1) - chunks(u)):
                    n = chunks(u) + c
                    wait(pe, pt_ev, n - 1)
                    for kt in range(4 * c, min(4 * c + 4, blocks(u))):
                        i = nc.tensor.transpose(pT[n % 2][:, kt % 4 * P:(kt % 4 + 1) * P],
                                                Pr[:, u % 2, kt * P:(kt + 1) * P], identf[:, :])
                    i.then_inc(pt_mm, 1)

            def ranks(gr):
                a, n = GROUPS[gr]
                pe.wait_ge(chosen_rdy, gr + 1)
                wait(pe, seen_rdy, gr)
                pe.wait_ge(tl_ev, n_tl(a + n - 1 + RANK_LAG))
                R_ = pM[:, 0:n * E].rearrange("p (a e) -> p a e", a=n)
                mm(R_, onesb[:, :], seen[:, gr:gr + 1, :].to_broadcast([P, n, E]), start=True, stop=False)
                for b in range(n - 1):
                    mm(R_[:, b + 1:, :], onesb[:, :], chosen[:, a + b:a + b + 1, :].to_broadcast([P, n - 1 - b, E]),
                       start=False, stop=False)
                mm(R_, before[:, :], chosen[:, a:a + n, :], start=False, stop=True).then_inc(rank_mm, 1)

            def weigh(u):
                pe.wait_ge(pt_ev, chunks(u + 1))
                wait(pe, x1_rdy, u)
                for kt in range(blocks(u)):
                    i = mm(pO[:, 0:D], PT[:, u % 2, kt * P:(kt + 1) * P], TL[:, keys_of(u)[0] + PAIR * kt, P:2 * P],
                           start=kt == 0, stop=kt == blocks(u) - 1)
                i.then_inc(pv_mm, 1)

            pe.wait_ge(ident_rdy, 1)
            transposes(-XT_LEAD)
            pe.wait_ge(wqk_in, 32)
            for c in range(FC):
                i = mm(pS[0][:, 0:P], wq_sb[:, c, :], wk_sb[:, c, :], start=c == 0, stop=c == FC - 1)
            i.then_inc(A_mm, 1)
            pe.wait_ge(wo_in, 16)
            wo_c = wo_sb.rearrange("p (q c) -> p c q", c=FC)
            for c in range(FC):
                nc.tensor.transpose(pT[c // 4][:, c % 4 * P:(c % 4 + 1) * P], wo_c[:, c, :],
                                    identf[:, :]).then_inc(woT_mm, 1)
            pe.wait_ge(wv_in, 16)
            pe.wait_ge(woT_rdy, 2)
            for c in range(FC):
                i = mm(pS[1][:, 0:P], wv_sb[:, c, :], woT[:, c, :], start=c == 0, stop=c == FC - 1)
            i.then_inc(M_mm, 1)
            pe.wait_ge(gw_in, 16)
            nc.tensor.transpose(pO[:, 0:E], gw_sb[:, :], identf[0:E, 0:E]).then_inc(gwT_mm, 1)
            pe.wait_ge(A_rdy, 1)
            pe.wait_ge(M_rdy, 1)
            pe.wait_ge(gwT_rdy, 1)
            pe.wait_ge(consts, N_CONST)

            for s in range(-XT_LEAD, LAST_SLOT):
                if has_xx(s) and s > -XT_LEAD:
                    transposes(s)
                if is_tile(s + S_LEAD):
                    scores(s + S_LEAD)
                if has_tl(s):
                    projections(s)
                if is_tile(s):
                    turn(s)
                if group_at(s, RANK_LAG) is not None:
                    ranks(group_at(s, RANK_LAG))
                if is_tile(s - PV_LAG):
                    weigh(s - PV_LAG)

            pe.wait_ge(seen_rdy, NG)
            pe.wait_ge(place_rdy, NG)
            mm(pM[:, 0:E], onesb[:, :], seen[:, NG, :], start=True, stop=True).then_inc(cnt_mm, 1)
            pe.wait_ge(list_rdy, 2)
            pe.wait_ge(w_in, 16 * (2 + H // P))

            def turn_x(m, j):
                pe.wait_ge(xt_in[j], 16 * (m + 1))
                nc.tensor.transpose(bank[j % 2][:, 0:P], xt[:, j, 0:D], identf[:, :]).then_inc(xT_mm, 1)

            def up(m, j, w):
                t = m * LANES + j
                pe.wait_ge(xT_rdy, t + 1)
                mm(bank[2 + j % 2], xTs[:, j % 2, :], WB[:, ds(w, 2 * H)], start=True, stop=True).then_inc(h_mm, 1)

            def turn_g(m, j):
                t = m * LANES + j
                pe.wait_ge(g_rdy, t + 1)
                for c in range(H // P):
                    i = nc.tensor.transpose(bank[4 + j % 2][:, c * P:(c + 1) * P], g[:, j % 2, c * P:(c + 1) * P],
                                            identf[:, :])
                i.then_inc(gT_mm, 1)

            def down(m, j, w):
                t = m * LANES + j
                pe.wait_ge(gT_rdy, t + 1)
                for c in range(H // P):
                    i = mm(bank[6 + j % 2][:, 0:D], gTs[:, j % 2, c * P:(c + 1) * P],
                           WB[:, ds(w + (2 * H + c * D), D)],
                           start=c == 0, stop=c == H // P - 1)
                i.then_inc(y_mm, 1)

            def body(m):
                static = isinstance(m, int)
                _, w = nc.values_load_multi_w_load_instructions(
                    wcol[0:1, ds(m * LANES, LIST0 + LANES)], engines=[pe.engine], min_val=0,
                    max_val=(E - 1) * WIDE, skip_runtime_bounds_check_because=IN_RANGE)
                for j in range(LANES):
                    t = m * LANES + j
                    up(m, j, w[LIST0 + j])
                    if not static or t + 1 < NT:
                        turn_x(m + (j + 1) // LANES, (j + 1) % LANES)
                    if not static or t >= 1:
                        turn_g(m + (j - 1) // LANES, (j - 1) % LANES)
                    if not static or t >= 2:
                        down(m + (j - 2) // LANES, (j - 2) % LANES, w[LIST0 + j - 2])
                return w

            turn_x(0, 0)
            body(0)
            with pe.Fori(1, M_TILES - 1) as m:
                body(m)
            w = body(M_TILES - 1)
            turn_g(M_TILES - 1, LANES - 1)
            for j in range(LANES - 2, LANES):
                pe.wait_ge(y_rdy, NT - LANES + j - 1)
                down(M_TILES - 1, j, w[LIST0 + j])

        @block.scalar
        def _(act):
            copy = nc.scalar.activation

            def out_xx(s):
                u, v = s + XT_LEAD, s - X2T_LAG
                act.wait_ge(xx_mm, n_xx(s))
                to = [u] * is_tile(u) + [N_TILES + v % 4] * is_tile(v)
                lo = 0 if is_tile(u) else P
                copy(XX[:, to[0]:to[-1] + 1:max(to[-1] - to[0], 1), :],
                     pM[:, lo:lo + len(to) * P].rearrange("p (a b) -> p a b", b=P), ACT.Copy).then_inc(xx_ev, 1)

            def out_tl(s):
                act.wait_ge(tl_mm, n_tl(s))
                lo, hi = 0 if is_tile(s + TV_LEAD) else 2 * P, 2 * P + E if is_tile(s - L_LAG) else 2 * P
                copy(TL[:, s + TV_LEAD, lo:hi], pM[:, lo:hi], ACT.Copy).then_inc(tl_ev, 1)

            def out_pt(u):
                for c in range(chunks(u + 1) - chunks(u)):
                    n = chunks(u) + c
                    w = (min(4 * c + 4, blocks(u)) - 4 * c) * P
                    act.wait_ge(pt_mm, n + 1)
                    copy(PT[:, u % 2, 4 * c * P:4 * c * P + w], pT[n % 2][:, 0:w], ACT.Copy).then_inc(pt_ev, 1)

            def exps(u):
                w = blocks(u) * P
                act.wait_ge(max_rdy, u + 1)
                copy(Pr[:, u % 2, 0:w], pS[u % 2][:, 0:w], ACT.Exp, bias=negmax[:, u:u + 1], scale=1.0,
                     accum_out=rowsum[:, u:u + 1]).then_inc(p_rdy, 1)

            for s in range(-XT_LEAD, LAST_SLOT + 1):
                if has_xx(s):
                    out_xx(s)
                if s == -XT_LEAD:
                    act.wait_ge(A_mm, 1)
                    copy(A_sb[:, :], pS[0][:, 0:P], ACT.Copy, scale=float(F_ATT) ** -0.5).then_inc(A_rdy, 1)
                if has_tl(s):
                    out_tl(s)
                if is_tile(s):
                    out_pt(s)
                if is_tile(s + S_LEAD):
                    exps(s + S_LEAD)
                gr = group_at(s, ROUTE_LAG)
                if gr is not None:
                    a, n = GROUPS[gr]
                    act.wait_ge(dlog_rdy, gr + 1)
                    copy(elog[:, a:a + n, :], dlog[:, a:a + n, :], ACT.Exp).then_inc(elog_rdy, 1)

            pad(act, range(E // 2, E))

            def silu(m, j):
                act.wait_ge(h_mm, m * LANES + j + 1)
                copy(sil[:, j % 2, :], bank[2 + j % 2][:, 0:H], ACT.Silu).then_inc(sil_rdy, 1)

            def out_g(m, j):
                act.wait_ge(gT_mm, m * LANES + j + 1)
                copy(gTs[:, j % 2, :], bank[4 + j % 2][:, 0:H], ACT.Copy).then_inc(gT_rdy, 1)

            silu(0, 0)
            for j in range(1, LANES):
                silu(0, j)
                out_g(0, j - 1)
            with act.Fori(1, M_TILES) as m:
                for j in range(LANES):
                    silu(m, j)
                    out_g(m + (j - 1) // LANES, (j - 1) % LANES)
            out_g(M_TILES - 1, LANES - 1)

        @block.vector
        def _(dve):
            v = nc.vector

            def stats1(u):
                v.bn_stats(bn1[:, u, :], X[:, token_tile(u), :]).then_inc(bn1_rdy, 1)

            def aggregate1(u):
                dve.wait_ge(bn1_rdy, u + 1)
                v.bn_aggr(mv1[:, u, :], bn1[:, u, :]).then_inc(mv1_rdy, 1)

            def norm1(u):
                dve.wait_ge(rstd1_rdy, u // STAT1_GROUP + 1)
                wait(dve, xx_mm, n_xx(u - 4 - XT_LEAD) if u >= 4 else 0)
                v.tensor_scalar(xn[:, u % 4, :], X[:, token_tile(u), :], mv1[:, u, 0:1], rstd1[:, u:u + 1],
                                ALU.subtract, ALU.mult).then_inc(xn_rdy, 1)

            def maximum(u):
                dve.wait_ge(s_mm, u + 1)
                v.tensor_reduce(negmax[:, u:u + 1], pS[u % 2][:, 0:blocks(u) * P], AX.X, ALU.max,
                                negate=True).then_inc(max_rdy, 1)

            def inverse(u):
                dve.wait_ge(p_rdy, u + 1)
                v.reciprocal(rinv[:, u:u + 1], rowsum[:, u:u + 1]).then_inc(rinv_rdy, 1)

            def attend(u):
                dve.wait_ge(rinv_rdy, u + 1)
                dve.wait_ge(pv_mm, u + 1)
                v.scalar_tensor_tensor(out=X[:, token_tile(u), :], in0=pO[:, 0:D], scalar=rinv[:, u:u + 1],
                                       in1=X[:, token_tile(u), :], op0=ALU.mult, op1=ALU.add).then_inc(x1_rdy, 1)

            def stats2(u):
                dve.wait_ge(x1_rdy, u + 1)
                v.bn_stats(bn2[:, u, :], X[:, token_tile(u), :]).then_inc(bn2_rdy, 1)

            def aggregate2(u):
                dve.wait_ge(bn2_rdy, u + 1)
                v.bn_aggr(mv2[:, u, :], bn2[:, u, :]).then_inc(mv2_rdy, 1)

            def norm2(u):
                dve.wait_ge(rstd2_rdy, u + 1)
                if u >= ROWS_RING and u == GROUPS[GROUPS_OF[u]][0]:
                    gr = GROUPS_OF[u - ROWS_RING]
                    dve.wait_ge(scattered[gr], 16 * K * GROUPS[gr][1])
                v.tensor_scalar(rows[:, u % ROWS_RING, :, 0:D],
                                X[:, token_tile(u):token_tile(u) + 1, :].to_broadcast([P, K, D]),
                                mv2[:, u, 0:1], rstd2[:, u:u + 1], ALU.subtract, ALU.mult).then_inc(x2_rdy, 1)

            def top_values(u):
                dve.wait_ge(tl_ev, n_tl(u + L_LAG))
                v.max(top[:, u, :], TL[:, u + L_LAG + TV_LEAD, 2 * P:]).then_inc(top_rdy, 1)

            def top_experts(u):
                dve.wait_ge(top_rdy, u + 1)
                v.max_index(topi[:, u, :], top[:, u, :], TL[:, u + L_LAG + TV_LEAD, 2 * P:]).then_inc(topi_rdy, 1)

            def route(gr):
                a, n = GROUPS[gr]
                t = slice(a, a + n)
                dve.wait_ge(topi_rdy, a + n)
                v.tensor_tensor(hot[:, t, :, :], topi[:, t, 0:K].unsqueeze(3).to_broadcast([P, n, K, E]),
                                iota8[:, :].unsqueeze(1).unsqueeze(1).to_broadcast([P, n, K, E]),
                                ALU.is_equal).then_inc(hot_rdy, 1)
                v.tensor_tensor(dlog[:, t, :], top[:, t, :], top[:, t, 0:1].to_broadcast([P, n, 8]),
                                ALU.subtract).then_inc(dlog_rdy, 1)
                dve.wait_ge(hot_rdy, gr + 1)
                v.tensor_tensor(chosen[:, t, :], hot[:, t, 0, :], hot[:, t, 1, :], ALU.add).then_inc(chosen_rdy, 1)
                dve.wait_ge(chosen_rdy, gr + 1)
                with nc.allow_low_precision("counts of at most 4"):
                    v.tensor_reduce(newc[:, gr, :], chosen[:, t, :].rearrange("p a e -> p e a"), AX.X,
                                    ALU.add).then_inc(newc_rdy, 1)
                dve.wait_ge(newc_rdy, gr + 1)
                v.tensor_tensor(seen[:, gr + 1, :], seen[:, gr, :], newc[:, gr, :], ALU.add).then_inc(seen_rdy, 1)

            def places(gr):
                a, n = GROUPS[gr]
                dve.wait_ge(rank_mm, gr + 1)
                v.tensor_tensor(place[:, a:a + n, :], pM[:, 0:n * E].rearrange("p (a e) -> p a e", a=n),
                                stretch0[:, :].unsqueeze(1).to_broadcast([P, n, E]), ALU.add).then_inc(place_rdy, 1)

            def place_rows(gr):
                a, n = GROUPS[gr]
                t = slice(a, a + n)
                r = slice(a % ROWS_RING, a % ROWS_RING + n)
                dve.wait_ge(place_rdy, gr + 1)
                v.tensor_tensor(picked[:, gr % 2, 0:n, :, :], hot[:, t, :, :],
                                place[:, t, :].unsqueeze(2).to_broadcast([P, n, K, E]),
                                ALU.mult).then_inc(picked_rdy, 1)
                dve.wait_ge(elog_rdy, gr + 1)
                v.tensor_reduce(esum[:, t], elog[:, t, :], AX.X, ALU.add).then_inc(esum_rdy, 1)
                for h in range(PAIR):
                    i0 = a % NU // PAIR
                    v.tensor_copy(rows[:, r.start + h:r.stop:PAIR, :, COL_DEST].bitcast(u32),
                                  dests[:, a // NU, h, i0:i0 + n // PAIR, :].bitcast(u32))
                dve.wait_ge(esum_rdy, gr + 1)
                v.reciprocal(einv[:, t], esum[:, t]).then_inc(einv_rdy, 1)
                dve.wait_ge(picked_rdy, gr + 1)
                with nc.allow_low_precision("row numbers, exact in float32"):
                    v.tensor_reduce(slots[:, t, :], picked[:, gr % 2, 0:n, :, :], AX.X, ALU.add)
                dve.wait_ge(einv_rdy, gr + 1)
                v.tensor_tensor(rows[:, r, :, COL_W], elog[:, t, 0:K], einv[:, t].unsqueeze(2).to_broadcast([P, n, K]),
                                ALU.mult).then_inc(row_rdy, 1)

            for s in range(-STAT1_LEAD, LAST_SLOT + 1):
                u1, u2 = s + STAT1_LEAD, s - X1_LAG
                if group_at(s, PLACE_LAG) is not None:
                    places(group_at(s, PLACE_LAG))
                if is_tile(u2):
                    inverse(u2)
                if is_tile(u1):
                    if u1 == 0:
                        dve.wait_ge(x_head, 32)
                    if u1 == 2 * PAIR:
                        dve.wait_ge(x_mid, 32)
                    if u1 == NU:
                        dve.wait_ge(x_tail, 32)
                    stats1(u1)
                if is_tile(u2):
                    attend(u2)
                if is_tile(u1):
                    aggregate1(u1)
                if is_tile(u2):
                    stats2(u2)
                if is_tile(s + S_LEAD):
                    maximum(s + S_LEAD)
                if is_tile(u2):
                    aggregate2(u2)
                if is_tile(s + NORM1_LEAD):
                    norm1(s + NORM1_LEAD)
                if is_tile(s - TOP_LAG):
                    top_values(s - TOP_LAG)
                if is_tile(s - NORM2_LAG):
                    norm2(s - NORM2_LAG)
                if is_tile(s - TOP_LAG):
                    top_experts(s - TOP_LAG)
                if s == -NORM1_LEAD:
                    for c in range(2):
                        dve.wait_ge(woT_mm, 4 * (c + 1))
                        v.tensor_copy(woT[:, 4 * c:4 * c + 4, :].rearrange("p c q -> p (c q)"),
                                      pT[c][:, :]).then_inc(woT_rdy, 1)
                    dve.wait_ge(M_mm, 1)
                    v.tensor_copy(M_sb[:, :], pS[1][:, 0:P]).then_inc(M_rdy, 1)
                    dve.wait_ge(gwT_mm, 1)
                    v.tensor_copy(gwT[:, :], pO[:, 0:E]).then_inc(gwT_rdy, 1)
                    dve.wait_ge(pads_rdy, N_PADS)
                if group_at(s, ROUTE_LAG) is not None:
                    route(group_at(s, ROUTE_LAG))
                if group_at(s, PLACE_LAG) is not None:
                    place_rows(group_at(s, PLACE_LAG))

            n_link = [0]

            def link(i):
                n_link[0] += 1
                i.then_inc(listing, 1)
                dve.wait_ge(listing, n_link[0])

            dve.wait_ge(cnt_mm, 1)
            link(v.tensor_copy(cnt[:, :], pM[0:1, 0:E]))
            v.tensor_tensor(pad0[:, :], cnt[:, :], stretch0[0:1, :], ALU.add).then_inc(list_rdy, 1)
            link(v.tensor_scalar(cnti[:, :], cnt[:, :], float(P - 1), None, ALU.add))
            link(v.tensor_scalar(nti[:, :], cnti[:, :], P.bit_length() - 1, None, ALU.logical_shift_right))
            link(v.tensor_copy(ntf[:, :], nti[:, :]))
            link(v.tensor_tensor_scan(ntcum[:, :], ntf[:, :], zero8[:, :], 0.0, ALU.add, ALU.add))
            link(v.tensor_tensor(past[:, :, :], ntcum[:, :].unsqueeze(1).to_broadcast([1, NT, E]),
                                 iotat[:, :].unsqueeze(2).to_broadcast([1, NT, E]), ALU.is_le))
            link(v.tensor_tensor(pastn[:, :, :], past[:, :, :], ntf[:, :].unsqueeze(1).to_broadcast([1, NT, E]), ALU.mult))
            v.tensor_reduce(e_of[:, :], past[:, :, :], AX.X, ALU.add)
            link(v.tensor_reduce(s_of[:, :], pastn[:, :, :], AX.X, ALU.add))
            v.tensor_scalar(wcol[:, LIST0:], e_of[:, :], float(E - 1), float(WIDE), ALU.min, ALU.mult)
            link(v.tensor_tensor(i_of[:, :], iotat[:, :], s_of[:, :], ALU.subtract))
            link(v.tensor_scalar(r_of[:, :], i_of[:, :], float(P), None, ALU.mult))
            v.scalar_tensor_tensor(out=row0[:, :], in0=e_of[:, :], scalar=float(STRETCH), in1=r_of[:, :],
                                   op0=ALU.mult, op1=ALU.add).then_inc(list_rdy, 1)

            def out_x(m, j):
                dve.wait_ge(xT_mm, m * LANES + j + 1)
                v.tensor_copy(xTs[:, j % 2, :], bank[j % 2][:, 0:P]).then_inc(xT_rdy, 1)

            def gated(m, j):
                dve.wait_ge(sil_rdy, m * LANES + j + 1)
                v.tensor_tensor(g[:, j % 2, :], sil[:, j % 2, :], bank[2 + j % 2][:, H:2 * H],
                                ALU.mult).then_inc(g_rdy, 1)

            def weighted(m, j):
                if not isinstance(m, int) or m >= 1:
                    dve.wait_ge(y_out[j], 16 * m)
                v.tensor_copy(ydest[:, j:j + 1], xt[:, j, COL_DEST:COL_DEST + 1].bitcast(u32))
                dve.wait_ge(y_mm, m * LANES + j + 1)
                v.tensor_scalar(ysb[:, j, :], bank[6 + j % 2][:, 0:D], xt[:, j, COL_W:COL_W + 1], None,
                                ALU.mult).then_inc(y_rdy, 1)

            def body(m):
                static = isinstance(m, int)
                for j in range(LANES):
                    if not static or m * LANES + j + 1 < NT:
                        out_x(m + (j + 1) // LANES, (j + 1) % LANES)
                    gated(m, j)
                    if not static or m * LANES + j >= 2:
                        weighted(m + (j - 2) // LANES, (j - 2) % LANES)

            out_x(0, 0)
            body(0)
            body(1)
            with dve.Fori(2, M_TILES - 1) as m:
                body(m)
            body(M_TILES - 1)
            for j in range(LANES - 2, LANES):
                weighted(M_TILES - 1, j)

            for c in range(NF):
                Xc = X[:, c * FIN:(c + 1) * FIN, :]
                dve.wait_ge(yf_in[c % ZF], 16 * K * (c // ZF + 1))
                v.tensor_tensor(Xc, Xc, yf[:, c % ZF, 0, :, :], ALU.add).then_inc(sum0, 1)
                dve.wait_ge(sum0, c + 1)
                v.tensor_tensor(Xc, Xc, yf[:, c % ZF, 1, :, :], ALU.add).then_inc(sum1, 1)


_INS = ["L0_attn_in_features", "L0_attn_w_q", "L0_attn_w_k", "L0_attn_w_v", "L0_attn_w_o",
        "L0_ffn_gate_w", "L0_ffn_w1", "L0_ffn_w2", "L0_ffn_w3"]
_OUT = (B, S, D)


def kernel(**inputs):
    import concourse.bacc as bacc
    from concourse.bass_utils import run_bass_kernel_spmd

    nc = bacc.Bacc("TRN2", target_bir_lowering=False, num_devices=1)
    arrays, args = {}, []
    for name in _INS:
        a = np.ascontiguousarray(inputs[name])
        arrays[name] = a
        args.append(nc.dram_tensor(name, a.shape, mybir.dt.from_np(a.dtype), kind="ExternalInput").ap())
    out = nc.dram_tensor("out", _OUT, mybir.dt.float32, kind="ExternalOutput").ap()
    build(nc, *args, out)
    result = run_bass_kernel_spmd(nc, [arrays], core_ids=[0])
    return result.results[0]["out"]
```

```python
from contextlib import ExitStack

import numpy as np

import concourse.bass as bass
from concourse import mybir

P = 128
B, S, D = 4, 1024, 128
E, H, K = 8, 256, 2
F_ATT = 1024
EPS = 1e-5
N_TOK = B * S
QT = S // P
PAIR = 2
NU = PAIR * QT
N_TILES = B * QT
FC = F_ATT // P
GROUPS = [(a, 4) for a in range(0, N_TILES - 8, 4)] + [(N_TILES - 8, 8)]
MOST = max(n for _, n in GROUPS)
NG = len(GROUPS)
HEAD, NEXT = 2, 4
ROWS_RING = 16
GROUPS_OF = {a + n: gr for gr, (a, n) in enumerate(GROUPS) for n in range(GROUPS[gr][1])}
ROW = D + 4
COL_DEST, COL_W = D, D + 1
STRETCH = N_TOK + P
LANES = 8
OUT_LANES = 2 * LANES
MOST_TILES = (K * N_TOK + E * (P - 1)) // P
NT = -(-MOST_TILES // LANES) * LANES
SPARE = NT - K * N_TOK // P
HALF = 4
ROWS_HALF = K * P * sum(n for _, n in GROUPS[:HALF + 1])
NT0 = (ROWS_HALF - E * (P - 1)) // P // LANES * LANES
LISTS = [(0, NT0), (NT0, NT)]
N_PARTS = 5
M0 = NT0 // LANES
XS_ROWS = E * STRETCH + SPARE * P
YB_ROWS = K * N_TOK + (E + SPARE) * P
MASK = -3.0e38
IN_RANGE = "counts add up to K * N_TOK, and the expert number of a list entry is clamped to E - 1"
PARTS = 2
WIDE = H // P * D
UP = PARTS * 2 * H // WIDE
LIST0 = 4

XT_LEAD, TV_LEAD, S_LEAD = 3, 2, 1
STAT1_LEAD, NORM1_LEAD, STAT1_GROUP = 9, 4, 4
PV_LAG, X1_LAG, NORM2_LAG, X2T_LAG, L_LAG, TOP_LAG = 1, 2, 3, 4, 5, 6
ROUTE_LAG, RANK_LAG, PLACE_LAG = 6, 7, 8


def build(nc, x, w_q, w_k, w_v, w_o, gate_w, w1, w2, w3, out):
    f32, bf16 = mybir.dt.float32, mybir.dt.bfloat16
    f32r = mybir.dt.float32r
    i32, u32 = mybir.dt.int32, mybir.dt.uint32
    ALU, ACT, AX = mybir.AluOpType, mybir.ActivationFunctionType, mybir.AxisListType
    ds = bass.ds

    xs = nc.dram_tensor("expert_rows", (XS_ROWS, ROW), f32, kind="Internal").ap()
    yb = nc.dram_tensor("choice_rows", (YB_ROWS, D), f32, kind="Internal").ap()

    ctx = ExitStack()
    with ctx:
        def sb(name, shape, dt=f32):
            return ctx.enter_context(nc.sbuf_tensor(name, shape, dt))

        def pb(name):
            return ctx.enter_context(nc.psum_tensor(name, [P, 512], f32))

        def sem(name):
            return ctx.enter_context(nc.semaphore(name))

        X = sb("X", [P, N_TILES, D])
        W13 = sb("W13", [P, E * PARTS * 2 * H], f32r)
        W13e = W13[:, :].rearrange("p (e s h) -> p e s h", e=E, s=PARTS)
        w2_sb = sb("w2_sb", [P, E * H // P * D])
        A_sb, M_sb = sb("A_sb", [P, P]), sb("M_sb", [P, P])
        gw_sb, gwT = sb("gw_sb", [E, D]), sb("gwT", [P, E])
        identf, identb = sb("identf", [P, P]), sb("identb", [P, P], bf16)
        maskb = sb("maskb", [P, P], bf16)
        before = sb("before", [P, P], bf16)
        onesb = sb("onesb", [P, P], bf16)
        halves = sb("halves", [P, STAT1_GROUP])
        iota8 = sb("iota8", [P, E])
        stretch0 = sb("stretch0", [P, E])
        dests = sb("dests", [P, B // PAIR, PAIR, QT, K])
        xn = sb("xn", [P, 4, D])
        XX = sb("XX", [P, N_TILES + 4, P])
        TL = sb("TL", [P, N_TILES + L_LAG + TV_LEAD, 2 * P + E])
        first = (NU + L_LAG + TV_LEAD) * (2 * P + E)
        TLf = TL[:, :, :].rearrange("p t c -> p (t c)")
        wq_sb, wk_sb, wo_sb, wv_sb = (TLf[:, first + n * F_ATT:first + (n + 1) * F_ATT] for n in range(4))
        wq_sb, wk_sb, wv_sb = (w.rearrange("p (c d) -> p c d", c=FC) for w in (wq_sb, wk_sb, wv_sb))
        Pr = sb("Pr", [P, 2, S])
        PT = sb("PT", [P, 2, S])
        woT = PT[:, 0, 0:FC * P].rearrange("p (c q) -> p c q", c=FC)
        negmax, rowsum, rinv = (sb(n, [P, N_TILES]) for n in ("negmax", "rowsum", "rinv"))
        bn1, bn2 = sb("bn1", [P, N_TILES, 6]), sb("bn2", [P, N_TILES, 6])
        mv1, mv2 = sb("mv1", [P, N_TILES, 2]), sb("mv2", [P, N_TILES, 2])
        ve1, ve2 = sb("ve1", [P, N_TILES]), sb("ve2", [P, N_TILES])
        rstd1, rstd2 = sb("rstd1", [P, N_TILES]), sb("rstd2", [P, N_TILES])
        rows = sb("rows", [P, ROWS_RING, K, ROW])
        top, topi = sb("top", [P, N_TILES, 8]), sb("topi", [P, N_TILES, 8], u32)
        dlog, elog = sb("dlog", [P, N_TILES, 8]), sb("elog", [P, N_TILES, 8])
        esum, einv = sb("esum", [P, N_TILES]), sb("einv", [P, N_TILES])
        hot = sb("hot", [P, N_TILES, K, E], bf16)
        chosen = sb("chosen", [P, N_TILES, E], bf16)
        newc, seen = sb("newc", [P, NG, E], bf16), sb("seen", [P, NG + 1, E], bf16)
        place = sb("place", [P, N_TILES, E])
        picked = sb("picked", [P, 2, MOST, K, E])
        slots = sb("slots", [P, N_TILES, K], u32)
        cnt, cnti, ntiles = sb("cnt", [1, 2, E]), sb("cnti", [1, 2, E], i32), sb("ntiles", [1, 2, E], i32)
        ntf, zero8 = sb("ntf", [1, 2, E]), sb("zero8", [1, E])
        cum = sb("cum", [1, 2, E + 1])
        taken = sb("taken", [1, 2, E + 1])
        new, jump, step = (sb(n, [1, 2, E]) for n in ("new", "jump", "step"))
        pad0 = sb("pad0", [1, E], i32)
        iotat = sb("iotat", [1, NT])
        past, pasts = sb("past", [1, NT, E]), sb("pasts", [1, NT, E])
        e_of, s_of, i_of, r_of = (sb(n, [1, NT]) for n in ("e_of", "s_of", "i_of", "r_of"))
        row0, wcol = sb("row0", [1, NT], i32), sb("wcol", [1, LIST0 + NT], i32)
        padrows = sb("padrows", [P, E + SPARE, ROW])
        xt = sb("xt", [P, LANES, ROW])
        xTh, xTl = sb("xTh", [P, 2, P], f32r), sb("xTl", [P, 2, P], f32r)
        sil, g = sb("sil", [P, 2, H]), sb("g", [P, 2, H])
        gTs = sb("gTs", [P, 2, H])
        ysb, ydest = sb("ysb", [P, OUT_LANES, D]), sb("ydest", [P, OUT_LANES], u32)
        w13_raw = ysb[:, 0:2 * 2 * H // D, :].rearrange("p (z a) d -> p z (a d)", z=2)
        FIN = 4
        NF = N_TILES // FIN
        ZF = 4
        yf = XX[:, 0:ZF * K * FIN, :].rearrange("p (z k i) d -> p z k i d", z=ZF, k=K)

        pS = [ctx.enter_context(nc.psum_tensor(f"scores{i}", [P, 1024], f32)) for i in range(2)]
        pT, (pM, pO) = [pb("turned0"), pb("turned1")], [pb("mixed"), pb("weighed")]
        bank = [pS[0][:, 0:512], pS[0][:, 512:], pS[1][:, 0:512], pS[1][:, 512:], *pT, pM, pO]

        x_head, x_next, x_mid, x_tail = sem("x_head"), sem("x_next"), sem("x_mid"), sem("x_tail")
        raw_in, split_hi, split_lo = [sem("raw_in0"), sem("raw_in1")], sem("split_hi"), sem("split_lo")
        wqk_in, wv_in, wo_in, gw_in, w_in = sem("wqk_in"), sem("wv_in"), sem("wo_in"), sem("gw_in"), sem("w_in")
        const0, ident_rdy, consts, pads_rdy = sem("const0"), sem("ident_rdy"), sem("consts"), sem("pads_rdy")
        A_mm, woT_mm, M_mm, gwT_mm = sem("A_mm"), sem("woT_mm"), sem("M_mm"), sem("gwT_mm")
        A_rdy, woT_rdy, M_rdy, gwT_rdy = sem("A_rdy"), sem("woT_rdy"), sem("M_rdy"), sem("gwT_rdy")
        bn1_rdy, mv1_rdy, ve1_rdy, rstd1_rdy = sem("bn1_rdy"), sem("mv1_rdy"), sem("ve1_rdy"), sem("rstd1_rdy")
        bn2_rdy, mv2_rdy, ve2_rdy, rstd2_rdy = sem("bn2_rdy"), sem("mv2_rdy"), sem("ve2_rdy"), sem("rstd2_rdy")
        xn_rdy, xx_mm, xx_ev, tl_mm, tl_ev = sem("xn_rdy"), sem("xx_mm"), sem("xx_ev"), sem("tl_mm"), sem("tl_ev")
        s_mm, max_rdy, p_rdy = sem("s_mm"), sem("max_rdy"), sem("p_rdy")
        pt_mm, pt_ev, pv_mm, rinv_rdy, x1_rdy = sem("pt_mm"), sem("pt_ev"), sem("pv_mm"), sem("rinv_rdy"), sem("x1_rdy")
        x2_rdy, top_rdy, topi_rdy = sem("x2_rdy"), sem("top_rdy"), sem("topi_rdy")
        dlog_rdy, elog_rdy, hot_rdy, chosen_rdy = sem("dlog_rdy"), sem("elog_rdy"), sem("hot_rdy"), sem("chosen_rdy")
        newc_rdy, seen_rdy, rank_mm, place_rdy, picked_rdy = sem("newc_rdy"), sem("seen_rdy"), sem("rank_mm"), sem("place_rdy"), sem("picked_rdy")
        esum_rdy, einv_rdy, row_rdy = sem("esum_rdy"), sem("einv_rdy"), sem("row_rdy")
        scattered = [sem(f"scattered{gr}") for gr in range(NG)]
        held = sem("held")
        listing, list_rdy, pad0_rdy, padded = sem("listing"), sem("list_rdy"), sem("pad0_rdy"), sem("padded")
        xt_in = [sem(f"xt_in{j}") for j in range(LANES)]
        y_out = [sem(f"y_out{q}") for q in range(OUT_LANES)]
        xTh_rdy = sem("xTh_rdy")
        xT_mm, xT_rdy, h_mm, sil_rdy, g_rdy = sem("xT_mm"), sem("xT_rdy"), sem("h_mm"), sem("sil_rdy"), sem("g_rdy")
        gT_mm, gT_rdy, y_mm, y_rdy = sem("gT_mm"), sem("gT_rdy"), sem("y_mm"), sem("y_rdy")
        yf_in = [sem(f"yf_in{j}") for j in range(ZF)]
        sum0, sum1, out_done = sem("sum0"), sem("sum1"), sem("out_done")
        N_CONST, N_PADS, M_TILES = 6 + K, 10, NT // LANES

        def is_tile(u):
            return 0 <= u < N_TILES

        def blocks(u):
            return u % NU // PAIR + 1

        def keys_of(u):
            return u // NU * NU + u % PAIR, u

        def chunks(u):
            return sum(-(-blocks(v) // 4) for v in range(u))

        def token_tile(u):
            return u // NU * NU + (u % PAIR) * QT + u % NU // PAIR

        def group_at(s, lag):
            return next((gr for gr, (a, n) in enumerate(GROUPS) if a + n - 1 + lag == s), None)

        def wait(eng, semaphore, count):
            if count > 0:
                eng.wait_ge(semaphore, count)

        def has_xx(s):
            return is_tile(s + XT_LEAD) or is_tile(s - X2T_LAG)

        def has_tl(s):
            return is_tile(s + TV_LEAD) or is_tile(s - L_LAG)

        def n_xx(s):
            return sum(has_xx(z) for z in range(-XT_LEAD, s + 1))

        def n_tl(s):
            return sum(has_tl(z) for z in range(-TV_LEAD, s + 1))

        def xx_apart(s):
            return s < N_TILES and (s < 0 or blocks(s) * P <= 512)

        def xx_bank(s):
            return pS[s % 2][:, 512:] if xx_apart(s) else pM[:, :]

        LAST_SLOT = N_TILES - 1 + PLACE_LAG
        assert LAST_SLOT + 1 - N_TILES == LANES
        FIRST_STORE = N_TILES + 3

        def product_bank(m, j):
            return pO if isinstance(m, int) and m == 0 else bank[6 + j % 2]
        block = ctx.enter_context(nc.Block())

        @block.sync
        def _(sp):
            xv = x.rearrange("b (i p) d -> p b i d", p=P)
            Xv = X[:, :, :].rearrange("p (b i) d -> p b i d", b=B)
            for b in range(PAIR):
                sp.dma_start(Xv[:, b, 0:HEAD, :], xv[:, b, 0:HEAD, :]).then_inc(x_head, 16)
            sp.dma_start(wq_sb, w_q.rearrange("(p c) i -> p c i", p=P)).then_inc(wqk_in, 16)
            sp.dma_start(wk_sb, w_k.rearrange("(p c) i -> p c i", p=P)).then_inc(wqk_in, 16)
            for b in range(PAIR):
                sp.dma_start(Xv[:, b, HEAD:NEXT, :], xv[:, b, HEAD:NEXT, :]).then_inc(x_next, 16)
            sp.dma_start(wo_sb, w_o).then_inc(wo_in, 16)
            sp.dma_start(wv_sb, w_v.rearrange("(p c) i -> p c i", p=P)).then_inc(wv_in, 16)
            sp.dma_start(gw_sb[:, :], gate_w).then_inc(gw_in, 16)
            for b in range(PAIR):
                sp.dma_start(Xv[:, b, NEXT:QT, :], xv[:, b, NEXT:QT, :]).then_inc(x_mid, 16)
            for b in range(PAIR, B):
                sp.dma_start(Xv[:, b, :, :], xv[:, b, :, :]).then_inc(x_tail, 16)
            sp.dma_start(w2_sb[:, :].rearrange("p (e d) -> p e d", d=D),
                         w2.rearrange("e (t p) d -> p (e t) d", p=P)).then_inc(w_in, 16)
            for e in range(E):
                if e >= 2:
                    sp.wait_ge(split_lo, e - 1)
                sp.dma_start(w13_raw[:, e % 2, 0:H], w1[e]).then_inc(raw_in[e % 2], 16)
                sp.dma_start(w13_raw[:, e % 2, H:2 * H], w3[e]).then_inc(raw_in[e % 2], 16)
            sp.wait_ge(pads_rdy, N_PADS)
            sp.dma_start(xs[E * STRETCH:XS_ROWS, :].rearrange("(j p) c -> p j c", p=P),
                         padrows[:, E:, :]).then_inc(padded, 16)

            def load(m, pads=()):
                _, firsts = nc.values_load_multi_w_load_instructions(
                    row0[0:1, ds(m * LANES, LANES)], engines=[sp.engine], min_val=0, max_val=XS_ROWS - P,
                    skip_runtime_bounds_check_because=IN_RANGE)
                for j, r in enumerate(firsts):
                    if not isinstance(m, int) or m >= 1:
                        sp.wait_ge(y_rdy, m * LANES + j - LANES + 1)
                    sp.dma_start(xt[:, j, :], xs[ds(r, P), :]).then_inc(xt_in[j], 16)
                    for e in range(j, len(pads), LANES):
                        sp.dma_start(xs[ds(pads[e], P), :], padrows[:, e, :]).then_inc(padded, 16)

            def rows_of(groups):
                for gr in groups:
                    sp.wait_ge(scattered[gr], 16 * K * GROUPS[gr][1])

            rows_of(range(HALF + 1))
            sp.wait_ge(list_rdy, 1)
            load(0)
            with sp.Fori(1, M0 - 1) as m:
                load(m)
            sp.wait_ge(pad0_rdy, 1)
            _, starts = nc.values_load_multi_w_load_instructions(
                pad0[0:1, :], engines=[sp.engine], min_val=0, max_val=XS_ROWS - P,
                skip_runtime_bounds_check_because=IN_RANGE)
            load(M0 - 1, starts)
            rows_of(range(HALF + 1, NG))
            sp.wait_ge(padded, 16 * (E + 1))
            sp.wait_ge(list_rdy, 2)
            with sp.Fori(M0, M_TILES) as m:
                load(m)

            for q in range(OUT_LANES):
                sp.wait_ge(y_out[q], 16 * len(range(q, NT, OUT_LANES)))
            yv = yb[0:K * N_TOK, :].rearrange("(k c p i) d -> p k c i d", k=K, c=NF, i=FIN)

            def fetch(c):
                for k in range(K):
                    sp.dma_start(yf[:, c % ZF, k, :, :], yv[:, k, c, :, :]).then_inc(yf_in[c % ZF], 16)

            for c in range(ZF):
                fetch(c)
            for c in range(ZF, NF):
                sp.wait_ge(sum1, c - ZF + 1)
                fetch(c)
            sp.wait_ge(out_done, 16 * NF)

        @block.gpsimd
        def _(pool):
            nc.gpsimd.memset(identf[:, :], 0.0).then_inc(const0, 1)
            pool.wait_ge(const0, 1)
            nc.gpsimd.affine_select(out=identf[:, :], in_=identf[:, :], compare_op=ALU.not_equal, fill=1.0,
                                    base=0, pattern=[[-1, P]], channel_multiplier=1).then_inc(ident_rdy, 1)
            nc.gpsimd.memset(halves[:, :], -0.5).then_inc(consts, 1)

            def rstd_1(u0):
                t = slice(u0, u0 + STAT1_GROUP)
                pool.wait_ge(mv1_rdy, u0 + STAT1_GROUP)
                nc.gpsimd.tensor_scalar_add(ve1[:, t], mv1[:, t, 1], EPS).then_inc(ve1_rdy, 1)
                pool.wait_ge(ve1_rdy, u0 // STAT1_GROUP + 1)
                nc.gpsimd.tensor_tensor(rstd1[:, t], ve1[:, t], halves[:, :], ALU.pow).then_inc(rstd1_rdy, 1)

            def rstd_2(u):
                pool.wait_ge(mv2_rdy, u + 1)
                nc.gpsimd.tensor_scalar_add(ve2[:, u:u + 1], mv2[:, u, 1:2], EPS).then_inc(ve2_rdy, 1)
                pool.wait_ge(ve2_rdy, u + 1)
                nc.gpsimd.tensor_tensor(rstd2[:, u:u + 1], ve2[:, u:u + 1], halves[:, 0:1],
                                        ALU.pow).then_inc(rstd2_rdy, 1)

            def more_constants():
                nc.gpsimd.memset(maskb[:, :], 0.0).then_inc(const0, 1)
                nc.gpsimd.memset(onesb[:, :], 1.0).then_inc(consts, 1)
                pool.wait_ge(const0, 2)
                pool.wait_ge(consts, 2)
                nc.gpsimd.affine_select(out=maskb[:, :], in_=maskb[:, :], compare_op=ALU.is_ge, fill=MASK,
                                        base=0, pattern=[[-1, P]], channel_multiplier=1).then_inc(consts, 1)
                nc.gpsimd.tensor_copy(identb[:, :], identf[:, :]).then_inc(consts, 1)
                nc.gpsimd.affine_select(out=before[:, :], in_=onesb[:, :], compare_op=ALU.is_gt, fill=0.0,
                                        base=0, pattern=[[1, P]], channel_multiplier=-1).then_inc(consts, 1)
                nc.gpsimd.memset(seen[:, 0, :], 0.0).then_inc(consts, 1)
                for k in range(K):
                    nc.gpsimd.iota(dests[:, :, :, :, k].rearrange("p a h (c i) -> p (a h c) i", i=FIN).bitcast(u32),
                                   [[FIN * P, NF], [1, FIN]],
                                   base=k * N_TOK, channel_multiplier=FIN).then_inc(consts, 1)
                nc.gpsimd.iota(iota8[:, :], [[1, E]], base=0, channel_multiplier=0,
                               allow_small_or_imprecise_dtypes=True).then_inc(pads_rdy, 1)
                nc.gpsimd.iota(stretch0[:, :], [[STRETCH, E]], base=0, channel_multiplier=0,
                               allow_small_or_imprecise_dtypes=True).then_inc(pads_rdy, 1)
                nc.gpsimd.iota(iotat[:, :], [[1, NT]], base=0, channel_multiplier=0,
                               allow_small_or_imprecise_dtypes=True).then_inc(pads_rdy, 1)
                nc.gpsimd.memset(zero8[:, :], 0.0).then_inc(pads_rdy, 1)
                nc.gpsimd.memset(cum[:, :, :], 0.0).then_inc(pads_rdy, 1)
                nc.gpsimd.memset(taken[:, :, :], 0.0).then_inc(pads_rdy, 1)
                nc.gpsimd.memset(wcol[:, 0:LIST0].bitcast(f32), 0.0).then_inc(pads_rdy, 1)
                nc.gpsimd.memset(rows[:, :, :, D:ROW], 0.0).then_inc(pads_rdy, 1)
                nc.gpsimd.memset(padrows[:, :, :], 0.0).then_inc(pads_rdy, 1)
                pool.wait_ge(pads_rdy, N_PADS - 1)
                nc.gpsimd.iota(padrows[:, :, COL_DEST].bitcast(u32), [[P, E + SPARE]], base=K * N_TOK,
                               channel_multiplier=1).then_inc(pads_rdy, 1)

            def scatter(gr, u, k):
                if (u, k) == (GROUPS[gr][0], 0):
                    pool.wait_ge(row_rdy, gr + 1)
                nc.gpsimd.indirect_dma_start(
                    xs, bass.IndirectOffsetOnAxis(ap=slots[:, u, k:k + 1], axis=0),
                    rows[:, u % ROWS_RING, k, :], None).then_inc(scattered[gr], 16)

            def store(r, q):
                pool.wait_ge(y_rdy, r * OUT_LANES + q + 1)
                if not isinstance(r, int):
                    pool.sem_inc(held, 1)
                nc.gpsimd.indirect_dma_start(
                    yb, bass.IndirectOffsetOnAxis(ap=ydest[:, q:q + 1], axis=0),
                    ysb[:, q, :], None).then_inc(y_out[q], 16)

            def split(e):
                pool.wait_ge(raw_in[e % 2], 32 * (e // 2 + 1))
                nc.gpsimd.tensor_copy(W13e[:, e, 0, :], w13_raw[:, e % 2, :]).then_inc(split_hi, 1)
                pool.wait_ge(split_hi, e + 1)
                nc.gpsimd.tensor_tensor(W13e[:, e, 1, :], w13_raw[:, e % 2, :], W13e[:, e, 0, :].bitcast(f32),
                                        ALU.subtract).then_inc(split_lo, 1)

            waiting, room = [], 0.0
            for s in range(-STAT1_LEAD, LAST_SLOT + 1):
                u = s + STAT1_LEAD
                if is_tile(u) and u % STAT1_GROUP == STAT1_GROUP - 1:
                    rstd_1(u - STAT1_GROUP + 1)
                if u == STAT1_GROUP - 1:
                    more_constants()
                if is_tile(s - X1_LAG):
                    rstd_2(s - X1_LAG)
                if s % 2 == 0 and 0 <= s < 2 * E:
                    split(s // 2)
                gr = group_at(s, PLACE_LAG)
                if gr is not None:
                    a, n = GROUPS[gr]
                    waiting += [(gr, v, k) for v in range(a, a + n) for k in range(K)]
                room = min(room + (0.55 * blocks(s) + 0.3 if is_tile(s) else 1.0 if s > 0 else 0.0), 3.0)
                while waiting and room >= 1:
                    scatter(*waiting.pop(0))
                    room -= 1
                if s >= FIRST_STORE:
                    store(0, s - FIRST_STORE)
            for t in range(LAST_SLOT + 1 - FIRST_STORE, NT0):
                store(t // OUT_LANES, t % OUT_LANES)
                for _ in range(min(2, len(waiting))):
                    scatter(*waiting.pop(0))
            with pool.Fori(NT0 // OUT_LANES, NT // OUT_LANES) as r:
                for q in range(OUT_LANES):
                    store(r, q)
            for q in range(NT % OUT_LANES):
                store(NT // OUT_LANES, q)

        @block.tensor
        def _(pe):
            mm = nc.tensor.matmul

            def mixed_read(s):
                if has_tl(s - 1):
                    pe.wait_ge(tl_ev, n_tl(s - 1))
                else:
                    wait(pe, xx_ev, n_xx(s - 1))
                gr = group_at(s - 1, RANK_LAG)
                if gr is not None:
                    pe.wait_ge(place_rdy, gr + 1)

            def transposes(s):
                if xx_apart(s):
                    wait(pe, xx_ev, n_xx(s - 2))
                else:
                    mixed_read(s)
                to = xx_bank(s)
                u, v = s + XT_LEAD, s - X2T_LAG
                if is_tile(u):
                    pe.wait_ge(xn_rdy, u + 1)
                    i = nc.tensor.transpose(to[:, 0:P], xn[:, u % 4, :], identf[:, :])
                if is_tile(v):
                    pe.wait_ge(x2_rdy, v + 1)
                    i = nc.tensor.transpose(to[:, P:2 * P], rows[:, v % ROWS_RING, 0, 0:D], identf[:, :])
                i.then_inc(xx_mm, 1)

            def scores(u):
                pe.wait_ge(tl_ev, n_tl(u - TV_LEAD))
                k0, w = keys_of(u)[0], blocks(u) * P
                for c in range(0, w, 512):
                    n = min(512, w - c) // P
                    first = k0 + PAIR * (c // P)
                    keys = XX[:, first:first + PAIR * (n - 1) + 1:PAIR, :]
                    mm(pS[u % 2][:, c:c + n * P], TL[:, u, 0:P], keys, start=True, stop=c + 512 < w)
                mm(pS[u % 2][:, w - P:w], identb[:, :], maskb[:, :], start=False, stop=True).then_inc(s_mm, 1)

            def projections(s):
                if xx_apart(s):
                    pe.wait_ge(xx_ev, n_xx(s - 1))
                    mixed_read(s)
                else:
                    pe.wait_ge(xx_ev, n_xx(s))
                    if not has_xx(s):
                        mixed_read(s)
                u, v = s + TV_LEAD, s - L_LAG
                if is_tile(u):
                    mm(pM[:, 0:P], A_sb[:, :], XX[:, u, :], start=True, stop=True)
                    i = mm(pM[:, P:2 * P], XX[:, u, :], M_sb[:, :], start=True, stop=True)
                if is_tile(v):
                    i = mm(pM[:, 2 * P:2 * P + E], XX[:, N_TILES + v % 4, :], gwT[:, :], start=True, stop=True)
                i.then_inc(tl_mm, 1)

            def turn(u):
                pe.wait_ge(p_rdy, u + 1)
                for c in range(chunks(u + 1) - chunks(u)):
                    n = chunks(u) + c
                    wait(pe, pt_ev, n - 1)
                    for kt in range(4 * c, min(4 * c + 4, blocks(u))):
                        i = nc.tensor.transpose(pT[n % 2][:, kt % 4 * P:(kt % 4 + 1) * P],
                                                Pr[:, u % 2, kt * P:(kt + 1) * P], identf[:, :])
                    i.then_inc(pt_mm, 1)

            def ranks(gr):
                a, n = GROUPS[gr]
                pe.wait_ge(chosen_rdy, gr + 1)
                wait(pe, seen_rdy, gr)
                pe.wait_ge(tl_ev, n_tl(a + n - 1 + RANK_LAG))
                R_ = pM[:, 0:n * E].rearrange("p (a e) -> p a e", a=n)
                if gr in (HALF, NG - 1):
                    pe.wait_ge(seen_rdy, gr + 1)
                    mm(pM[:, n * E:(n + 1) * E], onesb[:, :], seen[:, gr + 1, :], start=True, stop=True)
                mm(R_, onesb[:, :], seen[:, gr:gr + 1, :].to_broadcast([P, n, E]), start=True, stop=False)
                for b in range(n - 1):
                    mm(R_[:, b + 1:, :], onesb[:, :], chosen[:, a + b:a + b + 1, :].to_broadcast([P, n - 1 - b, E]),
                       start=False, stop=False)
                mm(R_, before[:, :], chosen[:, a:a + n, :], start=False, stop=True).then_inc(rank_mm, 1)

            def weigh(u):
                pe.wait_ge(pt_ev, chunks(u + 1))
                wait(pe, x1_rdy, u)
                for kt in range(blocks(u)):
                    i = mm(pO[:, 0:D], PT[:, u % 2, kt * P:(kt + 1) * P], TL[:, keys_of(u)[0] + PAIR * kt, P:2 * P],
                           start=kt == 0, stop=kt == blocks(u) - 1)
                i.then_inc(pv_mm, 1)

            pe.wait_ge(wqk_in, 32)
            for c in range(FC):
                i = mm(pS[0][:, 0:P], wq_sb[:, c, :], wk_sb[:, c, :], start=c == 0, stop=c == FC - 1)
            i.then_inc(A_mm, 1)
            pe.wait_ge(ident_rdy, 1)
            transposes(-XT_LEAD)
            pe.wait_ge(wo_in, 16)
            wo_c = wo_sb.rearrange("p (q c) -> p c q", c=FC)
            for c in range(FC):
                nc.tensor.transpose(pT[c // 4][:, c % 4 * P:(c % 4 + 1) * P], wo_c[:, c, :],
                                    identf[:, :]).then_inc(woT_mm, 1)
            pe.wait_ge(gw_in, 16)
            nc.tensor.transpose(pO[:, 0:E], gw_sb[:, :], identf[0:E, 0:E]).then_inc(gwT_mm, 1)
            pe.wait_ge(wv_in, 16)
            pe.wait_ge(woT_rdy, 2)
            for c in range(FC):
                i = mm(pS[1][:, 0:P], wv_sb[:, c, :], woT[:, c, :], start=c == 0, stop=c == FC - 1)
            i.then_inc(M_mm, 1)
            transposes(1 - XT_LEAD)
            pe.wait_ge(A_rdy, 1)
            pe.wait_ge(M_rdy, 1)
            pe.wait_ge(gwT_rdy, 1)
            pe.wait_ge(consts, N_CONST)

            def turn_x(m, j):
                pe.wait_ge(xt_in[j], 16 * (m + 1))
                nc.tensor.transpose(bank[j % 2][:, 0:P], xt[:, j, 0:D], identf[:, :]).then_inc(xT_mm, 1)

            def up(m, j, w):
                t = m * LANES + j
                pe.wait_ge(xT_rdy, t + 1)
                hi, lo = W13[:, ds(w * UP, 2 * H)], W13[:, ds(w * UP + 2 * H, 2 * H)]
                mm(bank[2 + j % 2], xTh[:, j % 2, :], hi, start=True, stop=False)
                mm(bank[2 + j % 2], xTh[:, j % 2, :], lo, start=False, stop=False)
                mm(bank[2 + j % 2], xTl[:, j % 2, :], hi, start=False, stop=True).then_inc(h_mm, 1)

            def turn_g(m, j):
                t = m * LANES + j
                pe.wait_ge(g_rdy, t + 1)
                for c in range(H // P):
                    i = nc.tensor.transpose(bank[4 + j % 2][:, c * P:(c + 1) * P], g[:, j % 2, c * P:(c + 1) * P],
                                            identf[:, :])
                i.then_inc(gT_mm, 1)

            def down(m, j, w):
                t = m * LANES + j
                pe.wait_ge(gT_rdy, t + 1)
                if isinstance(m, int) and m == 0:
                    wait(pe, y_rdy, t)
                    if t == 0:
                        pe.wait_ge(x1_rdy, N_TILES)
                for c in range(H // P):
                    i = mm(product_bank(m, j)[:, 0:D], gTs[:, j % 2, c * P:(c + 1) * P],
                           w2_sb[:, ds(w + c * D, D)],
                           start=c == 0, stop=c == H // P - 1)
                i.then_inc(y_mm, 1)

            def weights_of(m):
                _, w = nc.values_load_multi_w_load_instructions(
                    wcol[0:1, ds(m * LANES, LIST0 + LANES)], engines=[pe.engine], min_val=0,
                    max_val=(E - 1) * WIDE, skip_runtime_bounds_check_because=IN_RANGE)
                return w

            def step(m, j, w):
                static, t = isinstance(m, int), m * LANES + j
                m_is_0 = static and m == 0
                up(m, j, w[LIST0 + j])
                if m_is_0 and has_xx(N_TILES + j):
                    transposes(N_TILES + j)
                if not static or t + 2 < NT:
                    turn_x(m + (j + 2) // LANES, (j + 2) % LANES)
                if not static or t >= 1:
                    turn_g(m + (j - 1) // LANES, (j - 1) % LANES)
                if not static or t >= 2:
                    down(m + (j - 2) // LANES, (j - 2) % LANES, w[LIST0 + j - 2])
                if m_is_0 and has_tl(N_TILES + j):
                    projections(N_TILES + j)
                if m_is_0 and group_at(N_TILES + j, RANK_LAG) is not None:
                    ranks(group_at(N_TILES + j, RANK_LAG))

            for s in range(1 - XT_LEAD, N_TILES):
                if s > 1 - XT_LEAD:
                    transposes(s)
                if is_tile(s + S_LEAD):
                    scores(s + S_LEAD)
                if has_tl(s):
                    projections(s)
                if is_tile(s):
                    turn(s)
                if group_at(s, RANK_LAG) is not None:
                    ranks(group_at(s, RANK_LAG))
                if is_tile(s - PV_LAG):
                    weigh(s - PV_LAG)
            pe.wait_ge(list_rdy, 1)
            w = weights_of(0)
            weigh(N_TILES - 1)
            pe.wait_ge(w_in, 16)
            pe.wait_ge(split_lo, E)
            turn_x(0, 0)
            turn_x(0, 1)
            for j in range(LANES):
                step(0, j, w)
            pe.wait_ge(place_rdy, NG)
            w = weights_of(1)
            for j in range(LANES):
                step(1, j, w)
            with pe.Fori(2, M0) as m:
                w = weights_of(m)
                for j in range(LANES):
                    step(m, j, w)
            pe.wait_ge(list_rdy, 2)
            with pe.Fori(M0, M_TILES - 1) as m:
                w = weights_of(m)
                for j in range(LANES):
                    step(m, j, w)
            w = weights_of(M_TILES - 1)
            for j in range(LANES):
                step(M_TILES - 1, j, w)
            turn_g(M_TILES - 1, LANES - 1)
            for j in range(LANES - 2, LANES):
                pe.wait_ge(y_rdy, NT - LANES + j - 1)
                down(M_TILES - 1, j, w[LIST0 + j])

        @block.scalar
        def _(act):
            copy = nc.scalar.activation

            def out_xx(s):
                u, v = s + XT_LEAD, s - X2T_LAG
                act.wait_ge(xx_mm, n_xx(s))
                to = [u] * is_tile(u) + [N_TILES + v % 4] * is_tile(v)
                lo = 0 if is_tile(u) else P
                copy(XX[:, to[0]:to[-1] + 1:max(to[-1] - to[0], 1), :],
                     xx_bank(s)[:, lo:lo + len(to) * P].rearrange("p (a b) -> p a b", b=P), ACT.Copy).then_inc(xx_ev, 1)

            def out_tl(s):
                act.wait_ge(tl_mm, n_tl(s))
                lo, hi = 0 if is_tile(s + TV_LEAD) else 2 * P, 2 * P + E if is_tile(s - L_LAG) else 2 * P
                copy(TL[:, s + TV_LEAD, lo:hi], pM[:, lo:hi], ACT.Copy).then_inc(tl_ev, 1)

            def out_pt(u):
                for c in range(chunks(u + 1) - chunks(u)):
                    n = chunks(u) + c
                    w = (min(4 * c + 4, blocks(u)) - 4 * c) * P
                    act.wait_ge(pt_mm, n + 1)
                    copy(PT[:, u % 2, 4 * c * P:4 * c * P + w], pT[n % 2][:, 0:w], ACT.Copy).then_inc(pt_ev, 1)

            def exps(u):
                w = blocks(u) * P
                act.wait_ge(max_rdy, u + 1)
                copy(Pr[:, u % 2, 0:w], pS[u % 2][:, 0:w], ACT.Exp, bias=negmax[:, u:u + 1], scale=1.0,
                     accum_out=rowsum[:, u:u + 1]).then_inc(p_rdy, 1)

            def silu(m, j):
                act.wait_ge(h_mm, m * LANES + j + 1)
                copy(sil[:, j % 2, :], bank[2 + j % 2][:, 0:H], ACT.Silu).then_inc(sil_rdy, 1)

            def out_g(m, j):
                act.wait_ge(gT_mm, m * LANES + j + 1)
                copy(gTs[:, j % 2, :], bank[4 + j % 2][:, 0:H], ACT.Copy).then_inc(gT_rdy, 1)

            def exp_logits(gr):
                a, n = GROUPS[gr]
                act.wait_ge(dlog_rdy, gr + 1)
                copy(elog[:, a:a + n, :], dlog[:, a:a + n, :], ACT.Exp).then_inc(elog_rdy, 1)

            for s in range(-XT_LEAD, LAST_SLOT + 1):
                if s >= N_TILES:
                    silu(0, s - N_TILES)
                if has_xx(s):
                    out_xx(s)
                if s > N_TILES:
                    out_g(0, s - 1 - N_TILES)
                if s == -XT_LEAD:
                    act.wait_ge(A_mm, 1)
                    copy(A_sb[:, :], pS[0][:, 0:P], ACT.Copy, scale=float(F_ATT) ** -0.5).then_inc(A_rdy, 1)
                    act.wait_ge(woT_mm, FC)
                    copy(woT[:, FC // 2:, :].rearrange("p c q -> p (c q)"), pT[1][:, :], ACT.Copy).then_inc(woT_rdy, 1)
                if has_tl(s):
                    out_tl(s)
                if is_tile(s):
                    out_pt(s)
                if is_tile(s + S_LEAD):
                    exps(s + S_LEAD)
                if group_at(s, ROUTE_LAG) is not None:
                    exp_logits(group_at(s, ROUTE_LAG))

            with act.Fori(1, M_TILES) as m:
                for j in range(LANES):
                    silu(m, j)
                    out_g(m + (j - 1) // LANES, (j - 1) % LANES)
            out_g(M_TILES - 1, LANES - 1)

            ov = out.rearrange("b (c i p) d -> (b c) p i d", c=NF // B, i=FIN)
            for c in range(NF):
                act.wait_ge(sum1, c + 1)
                act.dma_start(ov[c], X[:, c * FIN:(c + 1) * FIN, :]).then_inc(out_done, 16)

        @block.vector
        def _(dve):
            v = nc.vector

            def stats1(u):
                v.bn_stats(bn1[:, u, :], X[:, token_tile(u), :]).then_inc(bn1_rdy, 1)

            def aggregate1(u):
                dve.wait_ge(bn1_rdy, u + 1)
                v.bn_aggr(mv1[:, u, :], bn1[:, u, :]).then_inc(mv1_rdy, 1)

            def norm1(u):
                dve.wait_ge(rstd1_rdy, u // STAT1_GROUP + 1)
                wait(dve, xx_mm, n_xx(u - 4 - XT_LEAD) if u >= 4 else 0)
                v.tensor_scalar(xn[:, u % 4, :], X[:, token_tile(u), :], mv1[:, u, 0:1], rstd1[:, u:u + 1],
                                ALU.subtract, ALU.mult).then_inc(xn_rdy, 1)

            def maximum(u):
                dve.wait_ge(s_mm, u + 1)
                v.tensor_reduce(negmax[:, u:u + 1], pS[u % 2][:, 0:blocks(u) * P], AX.X, ALU.max,
                                negate=True).then_inc(max_rdy, 1)

            def inverse(u):
                dve.wait_ge(p_rdy, u + 1)
                v.reciprocal(rinv[:, u:u + 1], rowsum[:, u:u + 1]).then_inc(rinv_rdy, 1)

            def attend(u):
                dve.wait_ge(rinv_rdy, u + 1)
                dve.wait_ge(pv_mm, u + 1)
                v.scalar_tensor_tensor(out=X[:, token_tile(u), :], in0=pO[:, 0:D], scalar=rinv[:, u:u + 1],
                                       in1=X[:, token_tile(u), :], op0=ALU.mult, op1=ALU.add).then_inc(x1_rdy, 1)

            def stats2(u):
                dve.wait_ge(x1_rdy, u + 1)
                v.bn_stats(bn2[:, u, :], X[:, token_tile(u), :]).then_inc(bn2_rdy, 1)

            def aggregate2(u):
                dve.wait_ge(bn2_rdy, u + 1)
                v.bn_aggr(mv2[:, u, :], bn2[:, u, :]).then_inc(mv2_rdy, 1)

            def norm2(u):
                dve.wait_ge(rstd2_rdy, u + 1)
                gr = GROUPS_OF.get(u - ROWS_RING)
                if gr is not None and u - ROWS_RING == GROUPS[gr][0]:
                    dve.wait_ge(scattered[gr], 16 * K * GROUPS[gr][1])
                v.tensor_scalar(rows[:, u % ROWS_RING, :, 0:D],
                                X[:, token_tile(u):token_tile(u) + 1, :].to_broadcast([P, K, D]),
                                mv2[:, u, 0:1], rstd2[:, u:u + 1], ALU.subtract, ALU.mult).then_inc(x2_rdy, 1)

            def top_values(u):
                dve.wait_ge(tl_ev, n_tl(u + L_LAG))
                v.max(top[:, u, :], TL[:, u + L_LAG + TV_LEAD, 2 * P:]).then_inc(top_rdy, 1)

            def top_experts(u):
                dve.wait_ge(top_rdy, u + 1)
                v.max_index(topi[:, u, :], top[:, u, :], TL[:, u + L_LAG + TV_LEAD, 2 * P:]).then_inc(topi_rdy, 1)

            def route(gr):
                a, n = GROUPS[gr]
                t = slice(a, a + n)
                dve.wait_ge(topi_rdy, a + n)
                v.tensor_tensor(hot[:, t, :, :], topi[:, t, 0:K].unsqueeze(3).to_broadcast([P, n, K, E]),
                                iota8[:, :].unsqueeze(1).unsqueeze(1).to_broadcast([P, n, K, E]),
                                ALU.is_equal).then_inc(hot_rdy, 1)
                v.tensor_tensor(dlog[:, t, :], top[:, t, :], top[:, t, 0:1].to_broadcast([P, n, 8]),
                                ALU.subtract).then_inc(dlog_rdy, 1)
                dve.wait_ge(hot_rdy, gr + 1)
                v.tensor_tensor(chosen[:, t, :], hot[:, t, 0, :], hot[:, t, 1, :], ALU.add).then_inc(chosen_rdy, 1)
                dve.wait_ge(chosen_rdy, gr + 1)
                with nc.allow_low_precision("counts of at most 4"):
                    v.tensor_reduce(newc[:, gr, :], chosen[:, t, :].rearrange("p a e -> p e a"), AX.X,
                                    ALU.add).then_inc(newc_rdy, 1)
                dve.wait_ge(newc_rdy, gr + 1)
                v.tensor_tensor(seen[:, gr + 1, :], seen[:, gr, :], newc[:, gr, :], ALU.add).then_inc(seen_rdy, 1)

            def places(gr):
                a, n = GROUPS[gr]
                dve.wait_ge(rank_mm, gr + 1)
                if gr in (HALF, NG - 1):
                    link(v.tensor_copy(cnt[:, gr // (NG - 1), :], pM[0:1, n * E:(n + 1) * E]))
                v.tensor_tensor(place[:, a:a + n, :], pM[:, 0:n * E].rearrange("p (a e) -> p a e", a=n),
                                stretch0[:, :].unsqueeze(1).to_broadcast([P, n, E]), ALU.add).then_inc(place_rdy, 1)

            def place_rows(gr):
                a, n = GROUPS[gr]
                t = slice(a, a + n)
                r = slice(a % ROWS_RING, a % ROWS_RING + n)
                dve.wait_ge(place_rdy, gr + 1)
                v.tensor_tensor(picked[:, gr % 2, 0:n, :, :], hot[:, t, :, :],
                                place[:, t, :].unsqueeze(2).to_broadcast([P, n, K, E]),
                                ALU.mult).then_inc(picked_rdy, 1)
                dve.wait_ge(elog_rdy, gr + 1)
                v.tensor_reduce(esum[:, t], elog[:, t, :], AX.X, ALU.add).then_inc(esum_rdy, 1)
                for h in range(PAIR):
                    i0 = a % NU // PAIR
                    v.tensor_copy(rows[:, r.start + h:r.stop:PAIR, :, COL_DEST].bitcast(u32),
                                  dests[:, a // NU, h, i0:i0 + n // PAIR, :].bitcast(u32))
                dve.wait_ge(esum_rdy, gr + 1)
                v.reciprocal(einv[:, t], esum[:, t]).then_inc(einv_rdy, 1)
                dve.wait_ge(picked_rdy, gr + 1)
                with nc.allow_low_precision("row numbers, exact in float32"):
                    v.tensor_reduce(slots[:, t, :], picked[:, gr % 2, 0:n, :, :], AX.X, ALU.add)
                dve.wait_ge(einv_rdy, gr + 1)
                v.tensor_tensor(rows[:, r, :, COL_W], elog[:, t, 0:K], einv[:, t].unsqueeze(2).to_broadcast([P, n, K]),
                                ALU.mult).then_inc(row_rdy, 1)

            n_link = [0]

            def link(i):
                n_link[0] += 1
                i.then_inc(listing, 1)
                dve.wait_ge(listing, n_link[0])

            def list_tiles(l, part):
                t0, t1 = LISTS[l]
                n, t = t1 - t0, slice(t0, t1)
                if part == 0:
                    if l == 1:
                        v.tensor_tensor(pad0[:, :], cnt[:, l, :], stretch0[0:1, :], ALU.add).then_inc(pad0_rdy, 1)
                    link(v.tensor_scalar(cnti[:, l, :], cnt[:, l, :], float(l * (P - 1)), None, ALU.add))
                    link(v.tensor_scalar(ntiles[:, l, :], cnti[:, l, :], P.bit_length() - 1, None, ALU.logical_shift_right))
                    link(v.tensor_copy(ntf[:, l, :], ntiles[:, l, :]))
                elif part == 1:
                    link(v.tensor_tensor(new[:, l, :], ntf[:, l, :], taken[:, l, 0:E], ALU.subtract))
                    link(v.tensor_tensor_scan(cum[:, l, 1:], new[:, l, :], zero8[:, :], 0.0, ALU.add, ALU.add))
                    if l == 0:
                        link(v.tensor_scalar(cum[:, l, 1:], cum[:, l, 1:], float(n), None, ALU.min))
                        link(v.tensor_tensor(taken[:, 1, 0:E], cum[:, l, 1:], cum[:, l, 0:E], ALU.subtract))
                elif part == 2:
                    held_by_list = taken[:, 1, 0:E] if l == 0 else new[:, l, :]
                    v.tensor_tensor(past[:, t, :], cum[:, l, 1:].unsqueeze(1).to_broadcast([1, n, E]),
                                    iotat[:, 0:n].unsqueeze(2).to_broadcast([1, n, E]), ALU.is_le)
                    link(v.tensor_tensor(jump[:, l, :], taken[:, l, 1:], taken[:, l, 0:E], ALU.subtract))
                    link(v.tensor_tensor(step[:, l, :], jump[:, l, :], held_by_list, ALU.subtract))
                    link(v.tensor_tensor(pasts[:, t, :], past[:, t, :],
                                         step[:, l, :].unsqueeze(1).to_broadcast([1, n, E]), ALU.mult))
                elif part == 3:
                    v.tensor_reduce(e_of[:, t], past[:, t, :], AX.X, ALU.add)
                    link(v.tensor_reduce(s_of[:, t], pasts[:, t, :], AX.X, ALU.add))
                else:
                    v.tensor_scalar(wcol[:, LIST0 + t0:LIST0 + t1], e_of[:, t], float(E - 1), float(WIDE),
                                    ALU.min, ALU.mult)
                    link(v.scalar_tensor_tensor(out=i_of[:, t], in0=s_of[:, t], scalar=taken[:, l, 0:1],
                                                in1=iotat[:, 0:n], op0=ALU.add, op1=ALU.add))
                    link(v.tensor_scalar(r_of[:, t], i_of[:, t], float(P), None, ALU.mult))
                    v.scalar_tensor_tensor(out=row0[:, t], in0=e_of[:, t], scalar=float(STRETCH), in1=r_of[:, t],
                                           op0=ALU.mult, op1=ALU.add).then_inc(list_rdy, 1)

            def out_x(m, j):
                dve.wait_ge(xT_mm, m * LANES + j + 1)
                v.tensor_copy(xTh[:, j % 2, :], bank[j % 2][:, 0:P]).then_inc(xTh_rdy, 1)

            def rest_x(m, j):
                dve.wait_ge(xTh_rdy, m * LANES + j + 1)
                v.tensor_tensor(xTl[:, j % 2, :], bank[j % 2][:, 0:P], xTh[:, j % 2, :].bitcast(f32),
                                ALU.subtract).then_inc(xT_rdy, 1)

            def gated(m, j):
                dve.wait_ge(sil_rdy, m * LANES + j + 1)
                v.tensor_tensor(g[:, j % 2, :], sil[:, j % 2, :], bank[2 + j % 2][:, H:2 * H],
                                ALU.mult).then_inc(g_rdy, 1)

            def weighted(r, q):
                m, j = r * (OUT_LANES // LANES) + q // LANES, q % LANES
                if not isinstance(r, int) or r >= 1:
                    dve.wait_ge(y_out[q], 16 * r)
                v.tensor_copy(ydest[:, q:q + 1], xt[:, j, COL_DEST:COL_DEST + 1].bitcast(u32))
                dve.wait_ge(y_mm, m * LANES + j + 1)
                v.tensor_scalar(ysb[:, q, :], product_bank(m, j)[:, 0:D], xt[:, j, COL_W:COL_W + 1], None,
                                ALU.mult).then_inc(y_rdy, 1)

            def tile_step(r, q):
                def of(q):
                    return r * (OUT_LANES // LANES) + q // LANES, q % LANES
                more = not isinstance(r, int) or r * OUT_LANES + q + 2 < NT
                if more:
                    out_x(*of(q + 2))
                gated(*of(q))
                if q >= 2:
                    weighted(r, q - 2)
                if more:
                    rest_x(*of(q + 2))

            for s in range(-STAT1_LEAD, LAST_SLOT + 1):
                u1, u2 = s + STAT1_LEAD, s - X1_LAG
                if group_at(s, PLACE_LAG) is not None:
                    places(group_at(s, PLACE_LAG))
                if is_tile(u2):
                    inverse(u2)
                if is_tile(u1):
                    if u1 == 0:
                        dve.wait_ge(x_head, 32)
                    if u1 == HEAD * PAIR:
                        dve.wait_ge(x_next, 32)
                    if u1 == NEXT * PAIR:
                        dve.wait_ge(x_mid, 32)
                    if u1 == NU:
                        dve.wait_ge(x_tail, 32)
                    stats1(u1)
                if is_tile(u2):
                    attend(u2)
                if is_tile(u1):
                    aggregate1(u1)
                if is_tile(u2):
                    stats2(u2)
                if is_tile(s + NORM1_LEAD):
                    norm1(s + NORM1_LEAD)
                if is_tile(s + S_LEAD):
                    maximum(s + S_LEAD)
                if is_tile(u2):
                    aggregate2(u2)
                if is_tile(s - TOP_LAG):
                    top_values(s - TOP_LAG)
                if is_tile(s - NORM2_LAG):
                    norm2(s - NORM2_LAG)
                if is_tile(s - TOP_LAG):
                    top_experts(s - TOP_LAG)
                if s == -NORM1_LEAD:
                    dve.wait_ge(woT_mm, FC // 2)
                    v.tensor_copy(woT[:, 0:FC // 2, :].rearrange("p c q -> p (c q)"), pT[0][:, :]).then_inc(woT_rdy, 1)
                if s == 1 - NORM1_LEAD:
                    dve.wait_ge(gwT_mm, 1)
                    v.tensor_copy(gwT[:, :], pO[:, 0:E]).then_inc(gwT_rdy, 1)
                    dve.wait_ge(M_mm, 1)
                    v.tensor_copy(M_sb[:, :], pS[1][:, 0:P]).then_inc(M_rdy, 1)
                    dve.wait_ge(pads_rdy, N_PADS)
                if group_at(s, ROUTE_LAG) is not None:
                    route(group_at(s, ROUTE_LAG))
                if group_at(s, PLACE_LAG) is not None:
                    place_rows(group_at(s, PLACE_LAG))
                part = s - (GROUPS[HALF][0] + GROUPS[HALF][1] - 1 + PLACE_LAG)
                if 0 <= part < N_PARTS:
                    list_tiles(0, part)
                if s == N_TILES:
                    for j in range(2):
                        out_x(0, j)
                        rest_x(0, j)
                if s >= N_TILES:
                    tile_step(0, s - N_TILES)

            for t in range(LANES, OUT_LANES + 2):
                tile_step(0, t)
                if t % 2 == 0 and (t - LANES) // 2 < N_PARTS:
                    list_tiles(1, (t - LANES) // 2)
            with dve.Fori(1, (NT - 2) // OUT_LANES) as r:
                for q in range(2, OUT_LANES + 2):
                    tile_step(r, q)
            last = (NT - 2) // OUT_LANES
            for q in range(2, NT - last * OUT_LANES):
                tile_step(last, q)
            for t in range(NT - 2, NT):
                weighted(t // OUT_LANES, t % OUT_LANES)

            for c in range(NF):
                Xc = X[:, c * FIN:(c + 1) * FIN, :]
                dve.wait_ge(yf_in[c % ZF], 16 * K * (c // ZF + 1))
                v.tensor_tensor(Xc, Xc, yf[:, c % ZF, 0, :, :], ALU.add).then_inc(sum0, 1)
                dve.wait_ge(sum0, c + 1)
                v.tensor_tensor(Xc, Xc, yf[:, c % ZF, 1, :, :], ALU.add).then_inc(sum1, 1)


_INS = ["L0_attn_in_features", "L0_attn_w_q", "L0_attn_w_k", "L0_attn_w_v", "L0_attn_w_o",
        "L0_ffn_gate_w", "L0_ffn_w1", "L0_ffn_w2", "L0_ffn_w3"]
_OUT = (B, S, D)


def kernel(**inputs):
    import concourse.bacc as bacc
    from concourse.bass_utils import run_bass_kernel_spmd

    nc = bacc.Bacc("TRN2", target_bir_lowering=False, num_devices=1)
    arrays, args = {}, []
    for name in _INS:
        a = np.ascontiguousarray(inputs[name])
        arrays[name] = a
        args.append(nc.dram_tensor(name, a.shape, mybir.dt.from_np(a.dtype), kind="ExternalInput").ap())
    out = nc.dram_tensor("out", _OUT, mybir.dt.float32, kind="ExternalOutput").ap()
    build(nc, *args, out)
    result = run_bass_kernel_spmd(nc, [arrays], core_ids=[0])
    return result.results[0]["out"]
```
